# Optimizing a Trainium2 kernel written in Bass

```python
import numpy as np
import jax
import jax.numpy as jnp

def _softmax(x, axis=-1):
    return jax.nn.softmax(x, axis=axis)

def _gelu(x):
    return jax.nn.gelu(x, approximate=True)

def _silu(x):
    return jax.nn.silu(x)

def _sigmoid(x):
    return jax.nn.sigmoid(x)

def _layernorm(x, axis=-1, eps=1e-05):
    m = jnp.mean(x, axis=axis, keepdims=True)
    v = jnp.var(x, axis=axis, keepdims=True)
    return (x - m) / jnp.sqrt(v + eps)

def _scatter_add(tgt, idx, src, axis=0):
    return tgt.at[idx].add(src)

def _segment_sum(src, seg, n):
    return jax.ops.segment_sum(src, seg, n)
kernel_name = 'mk_vit_tower_d1_tok_img256_r4_c4f0c9'

def setup_inputs(seed: int=0):
    np.random.seed(seed)
    _w = jnp.asarray

    def _rec_inputs():
        import jax
        import jax.numpy as jnp
        _rk = jax.random.key(seed)
        x = -0.000125008 + 0.999885 * jax.random.normal(jax.random.fold_in(_rk, 1), (2, 64, 64, 64), jnp.float32)
        return x
    x = _rec_inputs()

    def _L0_tok_setup():
        import jax, jax.numpy as jnp
        import numpy as np
        DIM = 64
        NH = 8
        WH, WW = (8, 8)

        def _rope_axis(x, axis):
            half = x.shape[-1]
            inv_freq = 1.0 / 10000.0 ** (jnp.arange(0, half, 2, dtype=jnp.float32) / half)
            pos = jnp.arange(x.shape[axis], dtype=jnp.float32)
            ang = pos[:, None] * inv_freq
            cos, sin = (jnp.cos(ang), jnp.sin(ang))
            shape = [1, 1, 1, ang.shape[-1]]
            shape[axis] = ang.shape[0]
            cos = cos.reshape(shape).astype(x.dtype)
            sin = sin.reshape(shape).astype(x.dtype)
            x1, x2 = (x[..., 0::2], x[..., 1::2])
            r1 = x1 * cos - x2 * sin
            r2 = x1 * sin + x2 * cos
            return jnp.stack([r1, r2], axis=-1).reshape(x.shape)

        def _rope2(x):
            half = x.shape[-1] // 2
            return jnp.concatenate([_rope_axis(x[..., :half], 1), _rope_axis(x[..., half:], 2)], axis=-1)
        key = jax.random.key(seed)
        ks = jax.random.split(key, 5)
        B, H, W, C = (32, 64, 64, DIM)
        s = 1.0 / np.sqrt(C)
        return {'x': jax.random.normal(ks[0], (B, H, W, C), dtype=jnp.float32), 'qkv_w': jax.random.uniform(ks[1], (3 * C, C), jnp.float32, -s, s), 'qkv_b': jax.random.uniform(ks[2], (3 * C,), jnp.float32, -s, s), 'proj_w': jax.random.uniform(ks[3], (C, C), jnp.float32, -s, s), 'proj_b': jax.random.uniform(ks[4], (C,), jnp.float32, -s, s)}
    _L0_tok_all = _L0_tok_setup()
    _L0_tok_in = {k: v for k, v in _L0_tok_all.items() if k in ('qkv_w', 'qkv_b', 'proj_w', 'proj_b')}
    del _L0_tok_all

    def _L0_attn_setup():
        import jax, jax.numpy as jnp
        import numpy as np
        S, B, D, H, DH = (128, 32, 64, 8, 32)
        LN_EPS = 1e-05

        def elu_p1(x):
            return jax.nn.elu(x) + 1.0

        def sum_norm(x):
            return x / jnp.sum(x, axis=-1, keepdims=True)

        def layer_norm(x, g, b):
            mu = jnp.mean(x, axis=-1, keepdims=True)
            var = jnp.mean(jnp.square(x - mu), axis=-1, keepdims=True)
            return (x - mu) * jax.lax.rsqrt(var + LN_EPS) * g + b

        def _fast_rnn_forward(x, slow_W, out_W, ln_g, ln_b):
            slen, bsz, _ = x.shape
            o = layer_norm(x, ln_g, ln_b)
            qkv = jnp.einsum('sbd,ed->sbe', o, slow_W)
            qkv = qkv.reshape(slen, bsz, H, 5 * DH + 2)
            q, k, v, rk, rv, beta, rbeta = jnp.split(qkv, [DH, 2 * DH, 3 * DH, 4 * DH, 5 * DH, 5 * DH + 1], axis=-1)
            beta = jax.nn.sigmoid(beta)
            rbeta = jax.nn.sigmoid(rbeta)
            q = sum_norm(elu_p1(q))
            k = sum_norm(elu_p1(k))
            rk = jax.nn.softmax(rk, axis=-1)

            def ff_step(W, inp):
                qt, kt, vt, bt = inp
                v_old = jnp.einsum('bhij,bhj->bhi', W, kt)
                W = W + (bt * (vt - v_old))[..., :, None] * kt[..., None, :]
                z = jnp.einsum('bhij,bhj->bhi', W, qt)
                return (W, z)
            W0 = jnp.zeros((bsz, H, DH, DH), x.dtype)
            _, z = jax.lax.scan(ff_step, W0, (q, k, v, beta))

            def rec_step(carry, inp):
                R, h = carry
                zt, kt, vt, bt = inp
                q_rec = jax.nn.softmax(h, axis=-1)
                v_old = jnp.einsum('bhij,bhj->bhi', R, kt)
                R = R + (bt * (vt - v_old))[..., :, None] * kt[..., None, :]
                h = zt + jnp.einsum('bhij,bhj->bhi', R, q_rec)
                return ((R, h), h)
            R0 = jnp.zeros((bsz, H, DH, DH), x.dtype)
            h0 = jnp.zeros((bsz, H, DH), x.dtype)
            _, hs = jax.lax.scan(rec_step, (R0, h0), (z, rk, rv, rbeta))
            out = hs.reshape(slen, bsz, H * DH)
            out = jnp.einsum('sbe,de->sbd', out, out_W)
            return x + out
        key = jax.random.key(seed)
        k1, k2, k3 = jax.random.split(key, 3)
        x = jax.random.normal(k1, (S, B, D), jnp.float32)
        slow_W = jax.random.normal(k2, (H * (5 * DH + 2), D), jnp.float32) * 0.02
        out_W = jax.random.normal(k3, (D, H * DH), jnp.float32) * 0.02
        ln_g = jnp.ones((D,), jnp.float32)
        ln_b = jnp.zeros((D,), jnp.float32)
        return {'x': x, 'slow_W': slow_W, 'out_W': out_W, 'ln_g': ln_g, 'ln_b': ln_b}
    _L0_attn_all = _L0_attn_setup()
    _L0_attn_in = {k: v for k, v in _L0_attn_all.items() if k in ('slow_W', 'out_W', 'ln_g', 'ln_b')}
    del _L0_attn_all

    def _L0_ffn_setup():
        import jax, jax.numpy as jnp
        import numpy as np
        B, T, IN_DIM = (64, 64, 64)
        HID, OUT_DIM = (128, 64)
        N_LAYERS, N_EXPERTS, N_SHARED = (2, 16, 1)
        key = jax.random.key(seed)
        ks = jax.random.split(key, 10)
        s = 0.02
        x = jax.random.normal(ks[0], (B, T, IN_DIM), dtype=jnp.float32)
        route_id = jax.random.randint(ks[1], (B,), 0, N_EXPERTS)
        Wi = jax.random.normal(ks[2], (HID, IN_DIM), dtype=jnp.float32) * s
        bi = jnp.zeros((HID,), dtype=jnp.float32)
        Wr = jax.random.normal(ks[3], (N_LAYERS, N_EXPERTS, HID, HID), dtype=jnp.float32) * s
        br = jax.random.normal(ks[4], (N_LAYERS, N_EXPERTS, HID), dtype=jnp.float32) * s
        Ws = jax.random.normal(ks[5], (N_LAYERS, N_SHARED, HID, HID), dtype=jnp.float32) * s
        bs = jax.random.normal(ks[6], (N_LAYERS, N_SHARED, HID), dtype=jnp.float32) * s
        Wo = jax.random.normal(ks[7], (OUT_DIM, HID), dtype=jnp.float32) * s
        bo = jnp.zeros((OUT_DIM,), dtype=jnp.float32)
        return {'x': x, 'route_id': route_id, 'Wi': Wi, 'bi': bi, 'Wr': Wr, 'br': br, 'Ws': Ws, 'bs': bs, 'Wo': Wo, 'bo': bo}
    _L0_ffn_all = _L0_ffn_setup()
    _L0_ffn_in = {k: v for k, v in _L0_ffn_all.items() if k in ('route_id', 'Wi', 'bi', 'Wr', 'br', 'Ws', 'bs', 'Wo', 'bo')}
    del _L0_ffn_all
    return {'x': x, 'L0_tok_qkv_w': _L0_tok_in['qkv_w'], 'L0_tok_qkv_b': _L0_tok_in['qkv_b'], 'L0_tok_proj_w': _L0_tok_in['proj_w'], 'L0_tok_proj_b': _L0_tok_in['proj_b'], 'L0_attn_slow_W': _L0_attn_in['slow_W'], 'L0_attn_out_W': _L0_attn_in['out_W'], 'L0_attn_ln_g': _L0_attn_in['ln_g'], 'L0_attn_ln_b': _L0_attn_in['ln_b'], 'L0_ffn_route_id': _L0_ffn_in['route_id'], 'L0_ffn_Wi': _L0_ffn_in['Wi'], 'L0_ffn_bi': _L0_ffn_in['bi'], 'L0_ffn_Wr': _L0_ffn_in['Wr'], 'L0_ffn_br': _L0_ffn_in['br'], 'L0_ffn_Ws': _L0_ffn_in['Ws'], 'L0_ffn_bs': _L0_ffn_in['bs'], 'L0_ffn_Wo': _L0_ffn_in['Wo'], 'L0_ffn_bo': _L0_ffn_in['bo']}

def reference(x, L0_tok_qkv_w, L0_tok_qkv_b, L0_tok_proj_w, L0_tok_proj_b, L0_attn_slow_W, L0_attn_out_W, L0_attn_ln_g, L0_attn_ln_b, L0_ffn_route_id, L0_ffn_Wi, L0_ffn_bi, L0_ffn_Wr, L0_ffn_br, L0_ffn_Ws, L0_ffn_bs, L0_ffn_Wo, L0_ffn_bo):
    import jax
    import jax.numpy as jnp

    def _L0_tok_ref(x, qkv_w, qkv_b, proj_w, proj_b):
        import jax, jax.numpy as jnp
        import numpy as np
        DIM = 64
        NH = 8
        WH, WW = (8, 8)

        def _rope_axis(x, axis):
            half = x.shape[-1]
            inv_freq = 1.0 / 10000.0 ** (jnp.arange(0, half, 2, dtype=jnp.float32) / half)
            pos = jnp.arange(x.shape[axis], dtype=jnp.float32)
            ang = pos[:, None] * inv_freq
            cos, sin = (jnp.cos(ang), jnp.sin(ang))
            shape = [1, 1, 1, ang.shape[-1]]
            shape[axis] = ang.shape[0]
            cos = cos.reshape(shape).astype(x.dtype)
            sin = sin.reshape(shape).astype(x.dtype)
            x1, x2 = (x[..., 0::2], x[..., 1::2])
            r1 = x1 * cos - x2 * sin
            r2 = x1 * sin + x2 * cos
            return jnp.stack([r1, r2], axis=-1).reshape(x.shape)

        def _rope2(x):
            half = x.shape[-1] // 2
            return jnp.concatenate([_rope_axis(x[..., :half], 1), _rope_axis(x[..., half:], 2)], axis=-1)
        B, H, W, C = x.shape
        hd = C // NH
        N = WH * WW
        xw = x.reshape(B, H // WH, WH, W // WW, WW, C).transpose(0, 1, 3, 2, 4, 5).reshape(-1, N, C)
        qkv = xw @ qkv_w.T + qkv_b
        qkv = qkv.reshape(-1, N, 3, NH, hd).transpose(2, 0, 3, 1, 4)
        q, k, v = (qkv[0], qkv[1], qkv[2])
        q = _rope2(q.reshape(-1, WH, WW, hd)).reshape(-1, NH, N, hd)
        k = _rope2(k.reshape(-1, WH, WW, hd)).reshape(-1, NH, N, hd)
        scale = hd ** (-0.5)
        attn = jax.nn.softmax(q * scale @ jnp.swapaxes(k, -2, -1), axis=-1)
        out = (attn @ v).transpose(0, 2, 1, 3).reshape(-1, N, C)
        out = out.reshape(B, H // WH, W // WW, WH, WW, C).transpose(0, 1, 3, 2, 4, 5).reshape(B, H * W, C)
        return out @ proj_w.T + proj_b

    def _L0_attn_ref(x, slow_W, out_W, ln_g, ln_b):
        import jax, jax.numpy as jnp
        import numpy as np
        S, B, D, H, DH = (128, 32, 64, 8, 32)
        LN_EPS = 1e-05

        def elu_p1(x):
            return jax.nn.elu(x) + 1.0

        def sum_norm(x):
            return x / jnp.sum(x, axis=-1, keepdims=True)

        def layer_norm(x, g, b):
            mu = jnp.mean(x, axis=-1, keepdims=True)
            var = jnp.mean(jnp.square(x - mu), axis=-1, keepdims=True)
            return (x - mu) * jax.lax.rsqrt(var + LN_EPS) * g + b

        def _fast_rnn_forward(x, slow_W, out_W, ln_g, ln_b):
            slen, bsz, _ = x.shape
            o = layer_norm(x, ln_g, ln_b)
            qkv = jnp.einsum('sbd,ed->sbe', o, slow_W)
            qkv = qkv.reshape(slen, bsz, H, 5 * DH + 2)
            q, k, v, rk, rv, beta, rbeta = jnp.split(qkv, [DH, 2 * DH, 3 * DH, 4 * DH, 5 * DH, 5 * DH + 1], axis=-1)
            beta = jax.nn.sigmoid(beta)
            rbeta = jax.nn.sigmoid(rbeta)
            q = sum_norm(elu_p1(q))
            k = sum_norm(elu_p1(k))
            rk = jax.nn.softmax(rk, axis=-1)

            def ff_step(W, inp):
                qt, kt, vt, bt = inp
                v_old = jnp.einsum('bhij,bhj->bhi', W, kt)
                W = W + (bt * (vt - v_old))[..., :, None] * kt[..., None, :]
                z = jnp.einsum('bhij,bhj->bhi', W, qt)
                return (W, z)
            W0 = jnp.zeros((bsz, H, DH, DH), x.dtype)
            _, z = jax.lax.scan(ff_step, W0, (q, k, v, beta))

            def rec_step(carry, inp):
                R, h = carry
                zt, kt, vt, bt = inp
                q_rec = jax.nn.softmax(h, axis=-1)
                v_old = jnp.einsum('bhij,bhj->bhi', R, kt)
                R = R + (bt * (vt - v_old))[..., :, None] * kt[..., None, :]
                h = zt + jnp.einsum('bhij,bhj->bhi', R, q_rec)
                return ((R, h), h)
            R0 = jnp.zeros((bsz, H, DH, DH), x.dtype)
            h0 = jnp.zeros((bsz, H, DH), x.dtype)
            _, hs = jax.lax.scan(rec_step, (R0, h0), (z, rk, rv, rbeta))
            out = hs.reshape(slen, bsz, H * DH)
            out = jnp.einsum('sbe,de->sbd', out, out_W)
            return x + out
        return _fast_rnn_forward(x, slow_W, out_W, ln_g, ln_b)

    def _L0_ffn_ref(x, route_id, Wi, bi, Wr, br, Ws, bs, Wo, bo):
        import jax, jax.numpy as jnp
        import numpy as np
        B, T, IN_DIM = (64, 64, 64)
        HID, OUT_DIM = (128, 64)
        N_LAYERS, N_EXPERTS, N_SHARED = (2, 16, 1)
        flat = x.reshape(-1, x.shape[-1])
        n_tok = flat.shape[0]
        route = jnp.repeat(route_id, n_tok // route_id.shape[0])
        h = jax.nn.relu(flat @ Wi.T + bi)
        n_layers, n_experts = (Wr.shape[0], Wr.shape[1])
        for l in range(n_layers):
            shared = (jnp.einsum('nd,shd->snh', h, Ws[l]) + bs[l][:, None, :]).mean(axis=0)
            routed = jnp.zeros_like(h)
            for e in range(n_experts):
                ye = h @ Wr[l, e].T + br[l, e]
                routed = routed + jnp.where((route == e)[:, None], ye, 0.0)
            h = jax.nn.relu(shared + routed + h)
        out = h @ Wo.T + bo
        return out.reshape(*x.shape[:-1], out.shape[-1])
    h = _L0_tok_ref(x, L0_tok_qkv_w, L0_tok_qkv_b, L0_tok_proj_w, L0_tok_proj_b)
    h = h + _L0_attn_ref(_layernorm(h, axis=-1), L0_attn_slow_W, L0_attn_out_W, L0_attn_ln_g, L0_attn_ln_b)
    h = h + _L0_ffn_ref(_layernorm(h, axis=-1), L0_ffn_route_id, L0_ffn_Wi, L0_ffn_bi, L0_ffn_Wr, L0_ffn_br, L0_ffn_Ws, L0_ffn_bs, L0_ffn_Wo, L0_ffn_bo)
    return h

_drawn_inputs = setup_inputs


def setup_inputs(seed=0):
    import zlib

    import numpy as np

    out = dict(_drawn_inputs(seed))
    spreads = {'L0_attn_ln_g': (1.0, 0.6),
     'L0_attn_ln_b': (0.0, 0.8),
     'L0_ffn_bi': (0.0, 0.484),
     'L0_ffn_bo': (0.0, 0.1)}
    factors = {'L0_attn_slow_W': 8.0,
     'L0_attn_out_W': 8.0,
     'L0_ffn_Wi': 2.741,
     'L0_ffn_Wr': 7.139,
     'L0_ffn_br': 8.0,
     'L0_ffn_Ws': 6.852,
     'L0_ffn_bs': 8.0}
    for name, (base, spread) in spreads.items():
        noise = np.random.default_rng([zlib.crc32(name.encode()), seed]).standard_normal(out[name].shape)
        drawn = base * np.exp(spread * noise) if base else spread * noise
        out[name] = jnp.asarray(drawn.astype(out[name].dtype))
    for name, factor in factors.items():
        out[name] = (out[name] * factor).astype(out[name].dtype)
    return out
```

```python
from contextlib import ExitStack

import concourse.bass as bass
import numpy as np
from concourse import mybir

F32 = mybir.dt.float32
ALU = mybir.AluOpType
ACT = mybir.ActivationFunctionType
AX = mybir.AxisListType

B, HH, WW, C = 2, 64, 64, 64
WIN = 8
NTOK = WIN * WIN
NWIN = (HH // WIN) * (WW // WIN)
TILES = NWIN // 2
NH, HD = 8, 8
RH, RD = 8, 32
RW = RH * RD
HID, NE, NL = 128, 16, 2
EPS = 1e-5
TOK = HH * WW
GROUPS = 16
BLK = 4
EW = HID + 1
CQK, CV, CRK = 0, 2 * RW, 4 * RW
WCOLS = 5 * RW + 2 * RH


def vit_tower(nc, x2, wqk, wv, bqk, bv, projT, projb, rot, mask_img, mask_head, ident_in,
              slowT, outT, ln_g, ln_b, route, wiT, bi, experts, shared, woT, bo, out):
    ctx = ExitStack()
    with ctx:
        def sb(name, shape):
            return ctx.enter_context(nc.sbuf_tensor(name, shape, F32))

        def bank(name):
            return ctx.enter_context(nc.psum_tensor(name, [128, 512], F32))

        IDN = sb("IDN", [128, 128])
        MIMG = sb("MIMG", [128, 2])
        MHEAD = sb("MHEAD", [128, NH])
        ROT = sb("ROT", [128, 16 * 128])
        WQK = sb("WQK", [128, C])
        BQK = sb("BQK", [128, 1])
        WROT = sb("WROT", [128, 16 * 128])
        QB = sb("QB", [128, 16])
        WV = sb("WV", [128, 2 * 64])
        PJ = sb("PJ", [128, 128])
        BV = sb("BV", [C, 1])
        BVB = sb("BVB", [C, 128])
        PROWB = sb("PROWB", [1, C])
        ONES = sb("ONES", [1, 128])
        PBIAS = sb("PBIAS", [128, 2 * C])
        WS = sb("WS", [C + 1, WCOLS])
        LNG = sb("LNG", [C, 1])
        LNB = sb("LNB", [C, 1])
        OW = sb("OW", [128, 2 * C])
        HALF = sb("HALF", [128, 4])
        NEG1 = sb("NEG1", [128, 1])
        ROUTE = ctx.enter_context(nc.sbuf_tensor("ROUTE", [1, 64], mybir.dt.int32))
        WI = sb("WI", [C, HID])
        BI = sb("BI", [HID, 1])
        EXP = sb("EXP", [128, NL * NE * EW])
        SHR = sb("SHR", [128, NL * EW])
        WO = sb("WO", [HID, C])
        BO = sb("BO", [128, 1])
        X2 = sb("X2", [128, TOK])
        Q2 = sb("Q2", [128, TOK])
        K2 = sb("K2", [128, TOK])
        HZT = sb("HZT", [128, B * TOK])
        XT = [sb(f"XT{p}", [128, 128]) for p in range(2)]
        QW = [sb(f"QW{p}", [128, 2 * 128]) for p in range(2)]
        KB = [[sb(f"KB{p}{w}", [128, 512]) for w in range(2)] for p in range(2)]
        MX = [sb(f"MX{w}", [128, NH]) for w in range(2)]
        SX = [sb(f"SX{w}", [128, 512]) for w in range(2)]
        PT = [sb(f"PT{w}", [128, 512]) for w in range(2)]
        VB = sb("VB", [128, 2 * 8 * 18])
        RDEN = sb("RDEN", [128, 16])
        CT = sb("CT", [128, 128])
        CTT = sb("CTT", [128, 128])
        H0 = sb("H0", [128, 128])
        ST1 = sb("ST1", [128, 12])
        MV1 = sb("MV1", [128, 4])
        PW1 = sb("PW1", [128, 4])
        RS1 = sb("RS1", [128, 4])
        RA = sb("RA", [128, 4])
        OH = sb("OH", [128, 128])
        RES = [sb(f"RES{p}", [128, 128]) for p in range(2)]
        OT = [sb(f"OT{p}", [C + 1, 256]) for p in range(2)]
        MR = sb("MR", [128, 2 * RH])
        BT = sb("BT", [128, 32])
        TH = sb("TH", [128, 32])
        BE = sb("BE", [128, 32])
        EQ = [sb(f"EQ{t}", [128, 512]) for t in range(2)]
        QK = sb("QK", [128, 2 * 512])
        RK = [sb(f"RK{p}", [128, 2 * RW]) for p in range(2)]
        V = [sb(f"V{p}", [128, 2 * 512]) for p in range(2)]
        PR = sb("PR", [128, 5 * RW])
        SM = sb("SM", [128, 48])
        RC = sb("RC", [128, 48])
        DT = sb("DT", [128, 40])
        NM = sb("NM", [128, 40])
        CC = [sb(f"CC{p}", [128, 16]) for p in range(2)]
        CF = [sb(f"CF{p}", [128, 32]) for p in range(2)]
        UU = [sb(f"UU{p}", [128, 16]) for p in range(2)]
        GG = [sb(f"GG{p}", [128, 8]) for p in range(2)]
        TA = sb("TA", [128, 8])
        HM = sb("HM", [128, 512])
        H12 = sb("H12", [128, 2 * RW])
        MH = sb("MH", [128, RH])
        QX = sb("QX", [128, RW])
        PQ = sb("PQ", [128, 3 * RW])
        DQ = sb("DQ", [128, 24])
        RQ = sb("RQ", [128, 8])
        TU = sb("TU", [128, 16])
        TB = sb("TB", [128, 8])
        HM2 = sb("HM2", [128, 1024])
        A1 = sb("A1", [128, 512])
        HT = sb("HT", [128, 512])
        HZ = sb("HZ", [128, 256])
        ST2 = sb("ST2", [128, 12])
        MV2 = sb("MV2", [128, 4])
        PW2 = sb("PW2", [128, 2])
        RS2 = sb("RS2", [128, 2])
        WSEL = [X2[:, p * 2048:p * 2048 + 8 * EW].rearrange("p (l b e) -> p l b e", l=NL, b=BLK)
                for p in range(2)]
        FA = Q2[:, 0:512]
        FB = Q2[:, 512:1024]
        FC = Q2[:, 1024:1536]
        FO = [K2[64:128, p * 512:(p + 1) * 512] for p in range(2)]

        S = [bank("S0"), bank("S1")]
        TP = bank("TP")
        CX = bank("CX")
        XA = bank("XA")
        XB = bank("XB")
        G = [bank("G0"), bank("G1")]

        names = """ldw ldx ldp lds lde stw zero zro1 wr wre qbm qbe qkp0 qkp1 qke0 qke1 bvb pbm pbe wsb wss
            shi setd xt0 xt1 qw kb0 kb1 vp vb sc0 sc1 mx0 mx1 sb0 sb1 ex0 ex1 tp0 tp1 pt0 pt1 pv0 pv1 rd cx ctp ctt pj h0
            bs1 bv1 pw1 rs1 ra oh res otp ot
            grk0 grk1 gqk0 gqk1 gv0 gv1 mr rsub0 rsub1 rk0 rk1 th eq0 eq1 el0 el1 vv0 vv1 pra prr sq sr rp rc be n1 n2
            n3 n4 n5 cc cf0 hm h1 mh qx qr pq dq rq t1 t2 cf1 cft hm2 a1 h2 htp ht ow yy bs2 bv2 pw2 rs2 zz ztp hz
            fsel0 fsel1 fh fhe fm0 fme0 fm1 fme1 fo foe fst0 fst1""".split()
        sem = {n: ctx.enter_context(nc.semaphore("s_" + n)) for n in names}

        def want(eng, name, n):
            if not isinstance(n, int) or n > 0:
                eng.wait_ge(sem[name], n)

        def v3(ap, b):
            return ap.rearrange("p (a b) -> p a b", b=b)

        def over(ap, k):
            return ap.unsqueeze(2).to_broadcast([ap.shape[0], ap.shape[1], k])

        def steps(eng, step, last=TILES):
            for s in range(4):
                step(eng, s, s // 2, s % 2, True, s > 0, s > 1)
            with eng.Fori(2, last // 2) as i:
                step(eng, i * 2, i, 0, True, True, True)
                step(eng, i * 2 + 1, i, 1, True, True, True)
            for s in range(last, TILES):
                step(eng, s, s // 2, s % 2, True, True, True)
            step(eng, TILES, 0, 0, False, True, True)
            step(eng, TILES + 1, 0, 1, False, False, True)

        block = ctx.enter_context(nc.Block())

        @block.sync
        def _(sp):
            sp.dma_start(WQK[:], wqk).then_inc(sem["ldw"], 16)
            sp.dma_start(BQK[:], bqk).then_inc(sem["ldw"], 16)
            sp.dma_start(ROT[:], rot).then_inc(sem["ldw"], 16)
            sp.dma_start(X2[:], x2).then_inc(sem["ldx"], 16)
            sp.dma_start(MIMG[:], mask_img).then_inc(sem["ldp"], 16)
            sp.dma_start(MHEAD[:], mask_head).then_inc(sem["ldp"], 16)
            sp.dma_start(IDN[:], ident_in).then_inc(sem["ldp"], 16)
            sp.wait_ge(sem["zero"], 1)
            for t in range(2):
                for e in range(2):
                    sp.dma_start(WV[64 * t:64 * t + 64, e * 64 + t * 32:e * 64 + t * 32 + 32],
                                 wv[:, e * 32:(e + 1) * 32]).then_inc(sem["lds"], 16)
                sp.dma_start(PJ[64 * t:64 * t + 64, t * C:(t + 1) * C], projT).then_inc(sem["lds"], 16)
            sp.dma_start(BV[:], bv).then_inc(sem["lds"], 16)
            sp.dma_start(PROWB[:], projb).then_inc(sem["lds"], 16)
            sp.dma_start(WS[0:C, :], slowT).then_inc(sem["lds"], 16)
            sp.dma_start(LNG[:], ln_g).then_inc(sem["lds"], 16)
            sp.dma_start(LNB[:], ln_b).then_inc(sem["lds"], 16)
            for c in range(2):
                sp.dma_start(OW[:, c * C:(c + 1) * C], outT[c * 128:(c + 1) * 128, :]).then_inc(sem["lds"], 16)
            sp.dma_start(WI[:], wiT).then_inc(sem["lde"], 16)
            sp.dma_start(BI[:], bi).then_inc(sem["lde"], 16)
            sp.dma_start(WO[:], woT).then_inc(sem["lde"], 16)
            sp.dma_start(BO[64:128, :], bo).then_inc(sem["lde"], 16)
            sp.dma_start(ROUTE[:], route).then_inc(sem["lde"], 16)
            sp.dma_start(SHR[:], shared).then_inc(sem["lde"], 16)
            sp.dma_start(EXP[:], experts).then_inc(sem["lde"], 16)

            def load_tile(sp, n, p):
                want(sp, "vp", n - 1)
                sp.dma_start(XT[p][:], x2[:, bass.ds(n * 128, 128)]).then_inc(sem[f"xt{p}"], 16)
            load_tile(sp, 0, 0)
            load_tile(sp, 1, 1)
            with sp.Fori(1, TILES // 2) as i:
                load_tile(sp, i * 2, 0)
                load_tile(sp, i * 2 + 1, 1)
            sp.wait_ge(sem["foe"], 1)
            sp.dma_start(out[0], FO[0]).then_inc(sem["fst0"], 16)
            sp.wait_ge(sem["foe"], 2)
            sp.dma_start(out[1], FO[1]).then_inc(sem["fst1"], 16)
            with sp.Fori(1, GROUPS // 2) as g:
                for p in range(2):
                    sp.wait_ge(sem["foe"], g * 2 + (p + 1))
                    sp.dma_start(out[bass.ds(g * 2 + p, 1)].rearrange("a c n -> (a c) n"), FO[p]).then_inc(sem[f"fst{p}"], 16)
            sp.wait_ge(sem["fst0"], 8 * GROUPS)
            sp.wait_ge(sem["fst1"], 8 * GROUPS)

        @block.gpsimd
        def _(pool):
            pool.wait_ge(sem["ldp"], 48)
            pool.wait_ge(sem["zro1"], 3)

            def prepare(pool, n, p):
                want(pool, "sc1", n - 1)
                nc.gpsimd.tensor_tensor(
                    QW[p][:].rearrange("p (w t q) -> p w t q", w=2, t=2),
                    Q2[:, bass.ds(n * 128, 128)].rearrange("p (w q) -> p w q", w=2).unsqueeze(2)
                    .to_broadcast([128, 2, 2, NTOK]),
                    MIMG[:].unsqueeze(1).unsqueeze(3).to_broadcast([128, 2, 2, NTOK]),
                    ALU.mult).then_inc(sem["qw"], 1)
                for w in range(2):
                    nc.gpsimd.tensor_tensor(
                        v3(KB[p][w][:], NTOK),
                        K2[:, bass.ds(n * 128 + w * 64, 64)].unsqueeze(1).to_broadcast([128, NH, NTOK]),
                        over(MHEAD[:], NTOK), ALU.mult).then_inc(sem[f"kb{w}"], 1)

            def rsqrt1(pool, n):
                pool.wait_ge(sem["pw1"], n + 1)
                want(pool, "oh", n)
                nc.gpsimd.tensor_tensor(RS1[:], PW1[:], HALF[:], ALU.pow).then_inc(sem["rs1"], 1)

            def products(pool, n, p):
                qk = QK[:]
                want(pool, "rp", n)
                pool.wait_ge(sem["el0"], n + 1)
                nc.gpsimd.tensor_tensor(PR[:, 2 * RW:3 * RW], qk[:, 0:RW], qk[:, RW:2 * RW], ALU.mult)
                pool.wait_ge(sem["el1"], n + 1)
                nc.gpsimd.tensor_tensor(v3(PR[:, 0:2 * RW], RW), v3(qk[:, 2 * RW:4 * RW], RW),
                                        qk[:, RW:2 * RW].unsqueeze(1).to_broadcast([128, 2, RW]), ALU.mult)
                nc.gpsimd.tensor_tensor(PR[:, 3 * RW:4 * RW], qk[:, 2 * RW:3 * RW], qk[:, 3 * RW:4 * RW],
                                        ALU.mult).then_inc(sem["pra"], 1)
                pool.wait_ge(sem["rk0"], n + 1)
                pool.wait_ge(sem["rk1"], n + 1)
                nc.gpsimd.tensor_tensor(PR[:, 4 * RW:5 * RW], RK[p][:, 0:RW], RK[p][:, RW:2 * RW],
                                        ALU.mult).then_inc(sem["prr"], 1)

            def first_state(pool, n, p):
                pool.wait_ge(sem["cc"], n + 1)
                pool.wait_ge(sem["vv0"], n + 1)
                want(pool, "h1", n)
                nc.gpsimd.tensor_tensor(v3(HM[:], RD), v3(V[p][:, 0:512], RD), over(CC[p][:], RD),
                                        ALU.mult).then_inc(sem["hm"], 1)

            def query_products(pool, n, p):
                pool.wait_ge(sem["qr"], n + 1)
                nc.gpsimd.tensor_tensor(v3(PQ[:, RW:3 * RW], RW), v3(RK[p][:], RW),
                                        PQ[:, 0:RW].unsqueeze(1).to_broadcast([128, 2, RW]),
                                        ALU.mult).then_inc(sem["pq"], 1)

            def second_state(pool, n, p):
                pool.wait_ge(sem["cf1"], n + 1)
                pool.wait_ge(sem["vv1"], n + 1)
                want(pool, "a1", n)
                nc.gpsimd.tensor_tensor(v3(HM2[:], RD), v3(V[p][:], RD), over(CF[p][:], RD),
                                        ALU.mult).then_inc(sem["hm2"], 1)

            def rsqrt2(pool, n):
                pool.wait_ge(sem["pw2"], n + 1)
                want(pool, "zz", n)
                nc.gpsimd.tensor_tensor(RS2[:], PW2[:], HALF[:, 0:2], ALU.pow).then_inc(sem["rs2"], 1)

            def step(pool, s, pair, p, a, b1, b2):
                if b2:
                    first_state(pool, s - 2, p)
                if b1:
                    products(pool, s - 1, 1 - p)
                if b2:
                    query_products(pool, s - 2, p)
                if b2:
                    second_state(pool, s - 2, p)
                if a:
                    rsqrt1(pool, s)
                if a and not (isinstance(s, int) and s + 1 == TILES):
                    prepare(pool, s + 1, 1 - p)
                if b2:
                    rsqrt2(pool, s - 2)

            pool.wait_ge(sem["qke0"], 16)
            pool.wait_ge(sem["qke1"], 16)
            prepare(pool, 0, 0)
            steps(pool, step, TILES - 2)

            pool.wait_ge(sem["lde"], 112)
            pool.wait_ge(sem["shi"], 1)
            pool.wait_ge(sem["ztp"], TILES)

            def select(pool, g, p):
                want(pool, "fme1", g - 1)
                for b in range(BLK):
                    e = pool.value_load(ROUTE[0:1, bass.ds(g * BLK + b, 1)], min_val=0, max_val=NE - 1)
                    last = nc.gpsimd.tensor_tensor(WSEL[p][:, 1, b, :], EXP[:, bass.ds(e * EW + NE * EW, EW)],
                                                   SHR[:, EW:2 * EW], ALU.add)
                last.then_inc(sem["fsel1"], 1)
            select(pool, 0, 0)
            select(pool, 1, 1)
            with pool.Fori(1, GROUPS // 2) as g:
                select(pool, g * 2, 0)
                select(pool, g * 2 + 1, 1)

        @block.scalar
        def _(act):
            a_ = nc.scalar.activation
            wrot = WROT[:].rearrange("p (v q t d) -> p v q t d", v=16, q=2, t=2)
            act.wait_ge(sem["zro1"], 1)
            for t in range(2):
                act.wait_ge(sem["wr"], t + 1)
                for half in range(2):
                    for qk in range(2):
                        last = a_(wrot[64 * t:64 * t + 64, half * 8:(half + 1) * 8, qk, t, :],
                                  G[half][64 * t:64 * t + 64, :].rearrange("p (v q d) -> p v q d", v=8, q=2)[:, :, qk, :],
                                  ACT.Copy)
                last.then_inc(sem["wre"], 1)
            act.wait_ge(sem["qbm"], 1)
            a_(QB[:], XA[:, 0:16], ACT.Copy).then_inc(sem["qbe"], 1)
            act.wait_ge(sem["qbe"], 1)
            for v in range(0, 16, 2):
                act.wait_ge(sem["qkp0"], v // 2 + 1)
                half, pos = v // 8, v % 8
                for qk, dst in ((0, Q2), (1, K2)):
                    d = dst[64 * half:64 * half + 64, :].rearrange("p (w r c) -> p w r c", r=8, c=8)
                    d = d[:, :, pos, :] if half == 0 else d[:, :, :, pos]
                    a_(d, v3(G[0][64 * qk:64 * qk + 64, :], 8), ACT.Identity,
                       bias=QB[64 * qk:64 * qk + 64, v:v + 1]).then_inc(sem["qke0"], 1)
            act.wait_ge(sem["pbm"], 1)
            for t in range(2):
                last = a_(PBIAS[:, t * C:(t + 1) * C], XB[:, 0:C], ACT.Copy)
            last.then_inc(sem["pbe"], 1)
            act.wait_ge(sem["zro1"], 4)

            vb = VB[:].rearrange("p (a c) -> p a c", c=18)

            def values(act, n):
                act.wait_ge(sem["vp"], n + 1)
                want(act, "pv1", n)
                for e in range(2):
                    last = a_(vb[64 * e:64 * e + 64, :, 9 * e:9 * e + 8],
                              v3(XA[64 * e:64 * e + 64, 0:128], 8), ACT.Copy)
                last.then_inc(sem["vb"], 1)

            def exps(act, n, w):
                act.wait_ge(sem[f"sb{w}"], n + 1)
                a_(SX[w][:], SX[w][:], ACT.Exp).then_inc(sem[f"ex{w}"], 1)

            def probsT(act, n, w):
                act.wait_ge(sem[f"tp{w}"], n + 1)
                want(act, f"pv{w}", n)
                a_(PT[w][:], TP[:], ACT.Copy).then_inc(sem[f"pt{w}"], 1)

            def ctxT(act, n):
                act.wait_ge(sem["ctp"], n + 1)
                want(act, "pj", n)
                a_(CTT[:], XA[:, 128:256], ACT.Copy).then_inc(sem["ctt"], 1)

            def obsT(act, n, p):
                act.wait_ge(sem["otp"], n + 1)
                want(act, "gv1", n - 1)
                a_(OT[p][0:C, :], XA[0:C, 0:256], ACT.Copy).then_inc(sem["ot"], 1)

            def rk_exp(act, n, p, t):
                act.wait_ge(sem[f"rsub{t}"], n + 1)
                a_(RK[p][:, t * RW:(t + 1) * RW], RK[p][:, t * RW:(t + 1) * RW], ACT.Exp).then_inc(sem[f"rk{t}"], 1)

            def gates(act, n):
                want(act, "be", n)
                a_(TH[:], BT[:], ACT.Tanh, scale=0.5).then_inc(sem["th"], 1)

            def qk_exp(act, n, t):
                act.wait_ge(sem[f"gqk{t}"], n + 1)
                want(act, f"el{t}", n)
                a_(EQ[t][:], G[t][:], ACT.Exp, bias=NEG1[:, 0:1]).then_inc(sem[f"eq{t}"], 1)

            def v_copy(act, n, p, t):
                act.wait_ge(sem[f"gv{t}"], n + 1)
                want(act, "hm2", n - 1)
                a_(V[p][:, t * 512:(t + 1) * 512], G[t][:], ACT.Copy).then_inc(sem[f"vv{t}"], 1)

            def query_exp(act, n):
                act.wait_ge(sem["qx"], n + 1)
                want(act, "dq", n)
                a_(PQ[:, 0:RW], QX[:], ACT.Exp).then_inc(sem["qr"], 1)

            def hT(act, n):
                act.wait_ge(sem["htp"], n + 1)
                want(act, "ow", n)
                a_(HT[:], XB[:], ACT.Copy).then_inc(sem["ht"], 1)

            def hzT(act, n):
                act.wait_ge(sem["ztp"], n + 1)
                a_(HZT[:].rearrange("p (t c) -> p t c", t=2)[:, :, bass.ds(n * 128, 128)],
                   v3(XB[:, 256:512], 128), ACT.Copy).then_inc(sem["hz"], 1)

            def step(act, s, pair, p, a, b1, b2):
                if a:
                    values(act, s)
                if b1:
                    rk_exp(act, s - 1, 1 - p, 0)
                    rk_exp(act, s - 1, 1 - p, 1)
                    gates(act, s - 1)
                if a:
                    exps(act, s, 0)
                if b1:
                    qk_exp(act, s - 1, 0)
                    qk_exp(act, s - 1, 1)
                if a:
                    exps(act, s, 1)
                    probsT(act, s, 0)
                if b2:
                    query_exp(act, s - 2)
                if a:
                    probsT(act, s, 1)
                if b1:
                    v_copy(act, s - 1, 1 - p, 0)
                    v_copy(act, s - 1, 1 - p, 1)
                if a:
                    ctxT(act, s)
                if b2:
                    hT(act, s - 2)
                if a:
                    obsT(act, s, p)
                if b2:
                    hzT(act, s - 2)

            act.wait_ge(sem["ldp"], 48)
            steps(act, step)

            def relus(act, g, p):
                act.wait_ge(sem["fh"], g + 1)
                want(act, "fm0", g)
                a_(FA, S[0][:], ACT.Relu, bias=BI[:, 0:1]).then_inc(sem["fhe"], 1)
                act.wait_ge(sem["fm0"], g + 1)
                want(act, "fm1", g)
                for b in range(BLK):
                    last = a_(FB[:, b * 128:(b + 1) * 128], S[1][:, b * 128:(b + 1) * 128], ACT.Relu,
                              bias=WSEL[p][:, 0, b, HID:HID + 1])
                last.then_inc(sem["fme0"], 1)
                act.wait_ge(sem["fm1"], g + 1)
                want(act, "fo", g)
                for b in range(BLK):
                    last = a_(FC[:, b * 128:(b + 1) * 128], TP[:, b * 128:(b + 1) * 128], ACT.Relu,
                              bias=WSEL[p][:, 1, b, HID:HID + 1])
                last.then_inc(sem["fme1"], 1)
            relus(act, 0, 0)
            relus(act, 1, 1)
            with act.Fori(1, GROUPS // 2) as g:
                relus(act, g * 2, 0)
                relus(act, g * 2 + 1, 1)

        @block.vector
        def _(dve):
            v_ = nc.vector
            v_.memset(WROT[:], 0.0).then_inc(sem["zro1"], 1)
            v_.memset(WV[:], 0.0)
            v_.memset(PJ[:], 0.0)
            v_.memset(ONES[:], 1.0).then_inc(sem["zero"], 1)
            v_.memset(VB[:], 0.0).then_inc(sem["zro1"], 1)
            v_.memset(HALF[:], -0.5)
            v_.memset(NEG1[:], -1.0)
            v_.memset(OT[0][C:C + 1, :], 1.0)
            v_.memset(OT[1][C:C + 1, :], 1.0).then_inc(sem["zro1"], 1)
            dve.wait_ge(sem["zro1"], 3)
            ones = VB[:].rearrange("p (a c) -> p a c", c=18)
            v_.memset(ones[0:64, :, 8:9], 1.0)
            v_.memset(ones[64:128, :, 17:18], 1.0).then_inc(sem["zro1"], 1)
            dve.wait_ge(sem["lds"], 16 * 13)
            v_.memset(BVB[:], 1.0).then_inc(sem["setd"], 1)
            dve.wait_ge(sem["setd"], 1)
            v_.tensor_scalar(BVB[:], BVB[:], BV[:, 0:1], None, ALU.mult).then_inc(sem["bvb"], 1)
            dve.wait_ge(sem["qbe"], 1)
            for v in range(1, 16, 2):
                dve.wait_ge(sem["qkp1"], v // 2 + 1)
                half, pos = v // 8, v % 8
                for qk, dst in ((0, Q2), (1, K2)):
                    d = dst[64 * half:64 * half + 64, :].rearrange("p (w r c) -> p w r c", r=8, c=8)
                    d = d[:, :, pos, :] if half == 0 else d[:, :, :, pos]
                    v_.tensor_scalar(d, v3(G[1][64 * qk:64 * qk + 64, :], 8),
                                     QB[64 * qk:64 * qk + 64, v:v + 1], None, ALU.add).then_inc(sem["qke1"], 1)
            dve.wait_ge(sem["wsb"], 3)
            v_.tensor_scalar(WS[C:C + 1, 0:512], S[0][C:C + 1, 0:512], 1.0, None, ALU.add)
            v_.tensor_copy(WS[C:C + 1, 512:1024], S[1][C:C + 1, 0:512])
            v_.tensor_copy(WS[C:C + 1, 1024:WCOLS], TP[C:C + 1, 0:WCOLS - 1024])
            v_.tensor_scalar(WS[0:C, :], WS[0:C, :], LNG[:, 0:1], None, ALU.mult).then_inc(sem["wss"], 1)
            dve.wait_ge(sem["lde"], 112)
            dve.wait_ge(sem["ldp"], 48)
            for l in range(NL):
                last = v_.tensor_tensor(SHR[:, l * EW:l * EW + HID], SHR[:, l * EW:l * EW + HID], IDN[:], ALU.add)
            last.then_inc(sem["shi"], 1)
            dve.wait_ge(sem["pbe"], 1)

            def rowmax(dve, n, w):
                dve.wait_ge(sem[f"sc{w}"], n + 1)
                v_.tensor_reduce(MX[w][:], v3(S[w][:], NTOK), AX.X, ALU.max).then_inc(sem[f"mx{w}"], 1)

            def rowsub(dve, n, w):
                dve.wait_ge(sem[f"mx{w}"], n + 1)
                want(dve, f"tp{w}", n)
                v_.tensor_tensor(v3(SX[w][:], NTOK), v3(S[w][:], NTOK), over(MX[w][:], NTOK),
                                 ALU.subtract).then_inc(sem[f"sb{w}"], 1)

            cx = CX[:, 0:144].rearrange("p (a c) -> p a c", c=9)

            def ctx_norm(dve, n):
                dve.wait_ge(sem["pv1"], n + 1)
                v_.reciprocal(RDEN[:], cx[:, :, 8]).then_inc(sem["rd"], 1)
                dve.wait_ge(sem["rd"], n + 1)
                want(dve, "ctp", n)
                v_.tensor_tensor(v3(CT[:], 8), cx[:, :, 0:8], over(RDEN[:], 8), ALU.mult).then_inc(sem["cx"], 1)

            def hidden0(dve, n):
                dve.wait_ge(sem["pj"], n + 1)
                v_.tensor_tensor(H0[:], XA[:, 256:384], PBIAS[:], ALU.add).then_inc(sem["h0"], 1)

            def stats1(dve, n):
                dve.wait_ge(sem["h0"], n + 1)
                for t in range(2):
                    last = v_.bn_stats(ST1[:, 6 * t:6 * t + 6], H0[:, 64 * t:64 * t + 64])
                last.then_inc(sem["bs1"], 1)

            def vars1(dve, n):
                dve.wait_ge(sem["pbe"], 1)
                dve.wait_ge(sem["bs1"], n + 1)
                for t in range(2):
                    last = v_.bn_aggr(MV1[:, 2 * t:2 * t + 2], ST1[:, 6 * t:6 * t + 6])
                last.then_inc(sem["bv1"], 1)
                dve.wait_ge(sem["bv1"], n + 1)
                want(dve, "rs1", n)
                mv = v3(MV1[:], 2)
                pw = v3(PW1[:], 2)
                v_.tensor_scalar(pw[:, :, 0], mv[:, :, 1], 1.0 + EPS, EPS * EPS, ALU.mult, ALU.add)
                v_.tensor_scalar(pw[:, :, 1], mv[:, :, 1], EPS, None, ALU.add).then_inc(sem["pw1"], 1)

            def normed1(dve, n, p):
                dve.wait_ge(sem["rs1"], n + 1)
                want(dve, "otp", n)
                for t in range(2):
                    last = v_.tensor_scalar(OH[:, 64 * t:64 * t + 64], H0[:, 64 * t:64 * t + 64],
                                            MV1[:, 2 * t:2 * t + 1], RS1[:, 2 * t:2 * t + 1],
                                            ALU.subtract, ALU.mult)
                mv, rs, ra = v3(MV1[:], 2), v3(RS1[:], 2), v3(RA[:], 2)
                last.then_inc(sem["oh"], 1)
                v_.tensor_scalar(ra[:, :, 0], rs[:, :, 1], 1.0, None, ALU.add)
                v_.scalar_tensor_tensor(ra[:, :, 1], mv[:, :, 0], -1.0, rs[:, :, 1], ALU.mult,
                                        ALU.mult).then_inc(sem["ra"], 1)

            def residual(dve, n, p):
                dve.wait_ge(sem["ra"], n + 1)
                for t in range(2):
                    last = v_.tensor_scalar(RES[p][:, 64 * t:64 * t + 64], H0[:, 64 * t:64 * t + 64],
                                            RA[:, 2 * t:2 * t + 1], RA[:, 2 * t + 1:2 * t + 2],
                                            ALU.mult, ALU.add)
                last.then_inc(sem["res"], 1)

            def rk_max(dve, n):
                for t in range(2):
                    dve.wait_ge(sem[f"grk{t}"], n + 1)
                    last = v_.tensor_reduce(MR[:, t * RH:(t + 1) * RH], v3(G[t][:, 0:RW], RD), AX.X, ALU.max)
                last.then_inc(sem["mr"], 1)

            def rk_sub(dve, n, p):
                dve.wait_ge(sem["mr"], n + 1)
                want(dve, "th", n)
                want(dve, "pq", n - 1)
                for t in range(2):
                    v_.tensor_copy(BT[:, t * 16:(t + 1) * 16], G[t][:, RW:RW + 16])
                    v_.tensor_tensor(v3(RK[p][:, t * RW:(t + 1) * RW], RD), v3(G[t][:, 0:RW], RD),
                                     over(MR[:, t * RH:(t + 1) * RH], RD), ALU.subtract).then_inc(sem[f"rsub{t}"], 1)

            def elu(dve, n, t):
                dve.wait_ge(sem[f"eq{t}"], n + 1)
                want(dve, "pra", n)
                v_.scalar_tensor_tensor(QK[:, t * 512:(t + 1) * 512], G[t][:], 1.0, EQ[t][:],
                                        ALU.max, ALU.min).then_inc(sem[f"el{t}"], 1)

            def sums(dve, n, p):
                dve.wait_ge(sem["el1"], n + 1)
                v_.tensor_reduce(SM[:, 0:32], v3(QK[:], RD), AX.X, ALU.add).then_inc(sem["sq"], 1)
                dve.wait_ge(sem["rk0"], n + 1)
                dve.wait_ge(sem["rk1"], n + 1)
                v_.tensor_reduce(SM[:, 32:48], v3(RK[p][:], RD), AX.X, ALU.add).then_inc(sem["sr"], 1)

            def dots(dve, n):
                dve.wait_ge(sem["th"], n + 1)
                v_.tensor_scalar(BE[:], TH[:], 0.5, 0.5, ALU.mult, ALU.add).then_inc(sem["be"], 1)
                dve.wait_ge(sem["sr"], n + 1)
                v_.reciprocal(RC[:], SM[:]).then_inc(sem["rc"], 1)
                dve.wait_ge(sem["prr"], n + 1)
                v_.tensor_reduce(DT[:], v3(PR[:], RD), AX.X, ALU.add).then_inc(sem["rp"], 1)

            def coefs(dve, n, p):
                be = BE[:].rearrange("p (t k h) -> p t k h", t=2, k=2)
                rc, dt, nm = v3(RC[:], 8), v3(DT[:], 8), v3(NM[:], 8)
                cf = CF[p][:].rearrange("p (t k h) -> p t k h", t=2, k=2)
                dve.wait_ge(sem["rp"], n + 1)
                dve.wait_ge(sem["rc"], n + 1)
                dve.wait_ge(sem["be"], n + 1)
                want(dve, "hm2", n - 1)
                v_.tensor_tensor(nm[:, 0:2], dt[:, 0:2], rc[:, 2:4], ALU.mult)
                v_.tensor_tensor(nm[:, 2:4], dt[:, 2:4], rc[:, 0:3:2], ALU.mult)
                v_.tensor_tensor(nm[:, 4], dt[:, 4], rc[:, 4], ALU.mult).then_inc(sem["n1"], 1)
                v_.tensor_tensor(v3(UU[p][:], 8), be[:, :, 1, :], rc[:, 4:6], ALU.mult)
                dve.wait_ge(sem["n1"], n + 1)
                v_.tensor_tensor(nm[:, 0:3], nm[:, 0:3], rc[:, 1:2].to_broadcast([128, 3, 8]), ALU.mult)
                v_.tensor_tensor(nm[:, 3], nm[:, 3], rc[:, 3], ALU.mult)
                v_.tensor_tensor(nm[:, 4], nm[:, 4], rc[:, 5], ALU.mult).then_inc(sem["n2"], 1)
                v_.tensor_scalar(CC[p][:, 8:16], be[:, 0, 1, :], 1.0 / RD, None, ALU.mult)
                dve.wait_ge(sem["n2"], n + 1)
                v_.tensor_tensor(nm[:, 0:3], nm[:, 0:3], be[:, 0:1, 0, :].to_broadcast([128, 3, 8]), ALU.mult)
                v_.tensor_tensor(cf[:, 1, 0, :], nm[:, 3], be[:, 1, 0, :], ALU.mult)
                v_.tensor_tensor(GG[p][:], nm[:, 4], be[:, 0, 1, :], ALU.mult).then_inc(sem["n3"], 1)
                dve.wait_ge(sem["n3"], n + 1)
                v_.tensor_copy(CC[p][:, 0:8], nm[:, 2]).then_inc(sem["cc"], 1)
                v_.tensor_tensor(TA[:], cf[:, 1, 0, :], nm[:, 1], ALU.mult).then_inc(sem["n4"], 1)
                dve.wait_ge(sem["n4"], n + 1)
                v_.tensor_tensor(cf[:, 0, 0, :], nm[:, 0], TA[:], ALU.subtract).then_inc(sem["cf0"], 1)

            def h_first(dve, n):
                dve.wait_ge(sem["hm"], n + 1)
                want(dve, "htp", n)
                v_.tensor_tensor(H12[:, 0:RW], HM[:, 0:RW], HM[:, RW:2 * RW], ALU.add).then_inc(sem["h1"], 1)
                dve.wait_ge(sem["h1"], n + 1)
                v_.tensor_reduce(MH[:], v3(H12[:, 0:RW], RD), AX.X, ALU.max).then_inc(sem["mh"], 1)

            def h_query(dve, n):
                dve.wait_ge(sem["mh"], n + 1)
                want(dve, "qr", n)
                v_.tensor_tensor(v3(QX[:], RD), v3(H12[:, 0:RW], RD), over(MH[:], RD),
                                 ALU.subtract).then_inc(sem["qx"], 1)

            def query_dots(dve, n, p):
                dve.wait_ge(sem["pq"], n + 1)
                v_.tensor_reduce(DQ[:], v3(PQ[:], RD), AX.X, ALU.add).then_inc(sem["dq"], 1)
                dve.wait_ge(sem["dq"], n + 1)
                v_.reciprocal(RQ[:], DQ[:, 0:8])
                v_.tensor_tensor(TU[:], UU[p][:], DQ[:, 8:24], ALU.mult).then_inc(sem["rq"], 1)
                dve.wait_ge(sem["rq"], n + 1)
                v_.tensor_tensor(v3(TU[:], 8), v3(TU[:], 8), RQ[:].unsqueeze(1).to_broadcast([128, 2, 8]),
                                 ALU.mult).then_inc(sem["t1"], 1)
                cf = CF[p][:].rearrange("p (t k h) -> p t k h", t=2, k=2)
                dve.wait_ge(sem["t1"], n + 1)
                dve.wait_ge(sem["cf0"], n + 1)
                v_.tensor_tensor(TB[:], TU[:, 8:16], GG[p][:], ALU.mult).then_inc(sem["t2"], 1)
                v_.tensor_copy(cf[:, 1, 1, :], TU[:, 8:16])
                dve.wait_ge(sem["t2"], n + 1)
                v_.tensor_tensor(cf[:, 0, 1, :], TU[:, 0:8], TB[:], ALU.subtract).then_inc(sem["cf1"], 1)

            def h_second(dve, n):
                dve.wait_ge(sem["hm2"], n + 1)
                v_.tensor_tensor(A1[:], HM2[:, 0:512], HM2[:, 512:1024], ALU.add).then_inc(sem["a1"], 1)
                dve.wait_ge(sem["a1"], n + 1)
                v_.tensor_tensor(H12[:, RW:2 * RW], A1[:, 0:RW], A1[:, RW:2 * RW], ALU.add).then_inc(sem["h2"], 1)

            hz = HZ[:].rearrange("p (t k c) -> p t k c", t=2, k=2)

            def stream(dve, n, p):
                dve.wait_ge(sem["ow"], n + 1)
                dve.wait_ge(sem["res"], n + 1)
                want(dve, "ztp", n)
                v_.tensor_tensor(hz[:, :, 1, :], v3(XB[:, 0:128], C), v3(RES[p][:], C), ALU.add).then_inc(sem["yy"], 1)
                dve.wait_ge(sem["yy"], n + 1)
                for t in range(2):
                    last = v_.bn_stats(ST2[:, 6 * t:6 * t + 6], hz[:, t, 1, :])
                last.then_inc(sem["bs2"], 1)
                dve.wait_ge(sem["pbe"], 1)
                dve.wait_ge(sem["bs2"], n + 1)
                for t in range(2):
                    last = v_.bn_aggr(MV2[:, 2 * t:2 * t + 2], ST2[:, 6 * t:6 * t + 6])
                last.then_inc(sem["bv2"], 1)
                dve.wait_ge(sem["bv2"], n + 1)
                want(dve, "rs2", n)
                v_.tensor_scalar(PW2[:], v3(MV2[:], 2)[:, :, 1], EPS, None, ALU.add).then_inc(sem["pw2"], 1)

            def normed2(dve, n):
                dve.wait_ge(sem["rs2"], n + 1)
                for t in range(2):
                    last = v_.tensor_scalar(hz[:, t, 0, :], hz[:, t, 1, :], MV2[:, 2 * t:2 * t + 1],
                                            RS2[:, t:t + 1], ALU.subtract, ALU.mult)
                last.then_inc(sem["zz"], 1)

            def step(dve, s, pair, p, a, b1, b2):
                if b1:
                    rk_max(dve, s - 1)
                if b2:
                    h_first(dve, s - 2)
                if b1:
                    rk_sub(dve, s - 1, 1 - p)
                if b2:
                    h_query(dve, s - 2)
                if a:
                    rowmax(dve, s, 0)
                    rowsub(dve, s, 0)
                if b1:
                    elu(dve, s - 1, 0)
                if a:
                    rowmax(dve, s, 1)
                    rowsub(dve, s, 1)
                if b1:
                    elu(dve, s - 1, 1)
                if b2:
                    query_dots(dve, s - 2, p)
                if b1:
                    sums(dve, s - 1, 1 - p)
                if a:
                    ctx_norm(dve, s)
                if b1:
                    dots(dve, s - 1)
                if a:
                    hidden0(dve, s)
                    stats1(dve, s)
                if b2:
                    h_second(dve, s - 2)
                if a:
                    vars1(dve, s)
                if b1:
                    coefs(dve, s - 1, 1 - p)
                if b2:
                    stream(dve, s - 2, p)
                if a:
                    normed1(dve, s, p)
                    residual(dve, s, p)
                if b2:
                    normed2(dve, s - 2)
            steps(dve, step)

            def select(dve, g, p):
                want(dve, "fme0", g - 1)
                for b in range(BLK):
                    e = dve.value_load(ROUTE[0:1, bass.ds(g * BLK + b, 1)], min_val=0, max_val=NE - 1)
                    last = v_.tensor_tensor(WSEL[p][:, 0, b, :], EXP[:, bass.ds(e * EW, EW)], SHR[:, 0:EW], ALU.add)
                last.then_inc(sem["fsel0"], 1)

            def finish(dve, g, pair, p):
                dve.wait_ge(sem["fo"], g + 1)
                want(dve, f"fst{p}", pair * 16)
                for b in range(BLK):
                    y = HZT[64:128, bass.ds(g * 512, 512)].rearrange("p (w n) -> p w n", w=8)
                    last = v_.scalar_tensor_tensor(
                        v3(FO[p][:, b * 128:(b + 1) * 128], 16), v3(CX[64:128, b * 128:(b + 1) * 128], 16),
                        BO[64:128, 0:1], y[:, :, b * 16:(b + 1) * 16], ALU.add, ALU.add)
                last.then_inc(sem["foe"], 1)
            dve.wait_ge(sem["hz"], TILES)
            dve.wait_ge(sem["sc1"], TILES)
            select(dve, 0, 0)
            select(dve, 1, 1)
            finish(dve, 0, 0, 0)
            finish(dve, 1, 0, 1)
            with dve.Fori(1, GROUPS // 2) as g:
                select(dve, g * 2, 0)
                select(dve, g * 2 + 1, 1)
                finish(dve, g * 2, g, 0)
                finish(dve, g * 2 + 1, g, 1)

        @block.tensor
        def _(pe):
            mm = nc.tensor.matmul
            tr = nc.tensor.transpose
            pe.wait_ge(sem["ldw"], 48)
            r5 = ROT[:].rearrange("p (v q t d) -> p v q t d", v=16, q=2, t=2)
            for t in range(2):
                for half in range(2):
                    last = mm(G[half][64 * t:64 * t + 64, :], WQK[:], r5[:, half * 8:(half + 1) * 8, :, t, :],
                              start=True, stop=True)
                last.then_inc(sem["wr"], 1)
            for v in range(16):
                last = mm(XA[:, v:v + 1], ROT[:, v * 128:(v + 1) * 128], BQK[:, 0:1], start=True, stop=True)
            last.then_inc(sem["qbm"], 1)
            pe.wait_ge(sem["wre"], 2)
            pe.wait_ge(sem["ldx"], 16)
            x5 = X2[:].rearrange("p (w r c) -> p w r c", r=8, c=8)
            for v in range(16):
                half, pos = v // 8, v % 8
                want(pe, f"qke{v % 2}", 2 * (v // 2))
                rhs = x5[:, :, pos, :] if half == 0 else x5[:, :, :, pos]
                mm(G[v % 2][:], WROT[:, v * 128:(v + 1) * 128], rhs, start=True, stop=True)\
                    .then_inc(sem[f"qkp{v % 2}"], 1)
            pe.wait_ge(sem["lds"], 16 * 13)
            for i, (b_, lo, hi) in enumerate(((S[0], 0, 512), (S[1], 512, 1024), (TP, 1024, WCOLS))):
                mm(b_[C:C + 1, 0:hi - lo], LNB[:, 0:1], WS[0:C, lo:hi], start=True, stop=True).then_inc(sem["wsb"], 1)
            pe.wait_ge(sem["bvb"], 1)
            pe.wait_ge(sem["zero"], 1)
            mm(XB[:, 0:C], BVB[:], PJ[0:C, 0:C], start=True, stop=False)
            mm(XB[:, 0:C], ONES[:], PROWB[:], start=False, stop=True).then_inc(sem["pbm"], 1)
            pe.wait_ge(sem["zro1"], 4)
            pe.wait_ge(sem["wss"], 1)
            pe.wait_ge(sem["ldp"], 48)

            def values(pe, n, pair, p):
                pe.wait_ge(sem[f"xt{p}"], pair * 16 + 16)
                want(pe, "ot", n)
                for w in range(2):
                    for e in range(2):
                        last = mm(XA[64 * e:64 * e + 64, w * 64:(w + 1) * 64], XT[p][:, w * 64:(w + 1) * 64],
                                  WV[:, e * 64:(e + 1) * 64], start=True, stop=True)
                last.then_inc(sem["vp"], 1)

            def scores(pe, n, p, w):
                pe.wait_ge(sem["qw"], n + 1)
                pe.wait_ge(sem[f"kb{w}"], n + 1)
                want(pe, f"sb{w}", n)
                mm(S[w][:], QW[p][:, w * 128:(w + 1) * 128], KB[p][w][:], start=True, stop=True)\
                    .then_inc(sem[f"sc{w}"], 1)

            def probsT(pe, n, w):
                pe.wait_ge(sem[f"ex{w}"], n + 1)
                want(pe, f"pt{1 - w}", n + w)
                for j in range(4):
                    last = tr(TP[:, j * 128:(j + 1) * 128], SX[w][:, j * 128:(j + 1) * 128], IDN[:])
                last.then_inc(sem[f"tp{w}"], 1)

            vb = VB[:].rearrange("p (w t j c) -> p w t j c", w=2, t=2, j=4)
            cx = CX[:, 0:144].rearrange("p (t j c) -> p t j c", t=2, j=4)

            def attend(pe, n, w):
                pe.wait_ge(sem[f"pt{w}"], n + 1)
                if w == 0:
                    pe.wait_ge(sem["vb"], n + 1)
                    want(pe, "cx", n)
                for t in range(2):
                    for j in range(4):
                        last = mm(cx[64 * w:64 * w + 64, t, j, :], PT[w][:, j * 128 + t * 64:j * 128 + t * 64 + 64],
                                  vb[:, w, t, j, :], start=True, stop=True)
                last.then_inc(sem[f"pv{w}"], 1)

            def ctxT(pe, n):
                pe.wait_ge(sem["cx"], n + 1)
                tr(XA[:, 128:256], CT[:], IDN[:]).then_inc(sem["ctp"], 1)

            def project(pe, n):
                pe.wait_ge(sem["ctt"], n + 1)
                mm(XA[:, 256:384], CTT[:], PJ[:], start=True, stop=True).then_inc(sem["pj"], 1)

            def obsT(pe, n):
                pe.wait_ge(sem["ldp"], 48)
                pe.wait_ge(sem["oh"], n + 1)
                for t in range(2):
                    last = tr(XA[0:C, t * 128:(t + 1) * 128], OH[:, t * C:(t + 1) * C], IDN[:])
                last.then_inc(sem["otp"], 1)

            def slow(pe, n, p, what, t):
                lo, wide = {"rk": (CRK, RW + 2 * RH), "qk": (CQK, 512), "v": (CV, 512)}[what]
                if what == "rk":
                    pe.wait_ge(sem["ot"], n + 1)
                    want(pe, f"vv{t}", n)
                elif what == "qk":
                    pe.wait_ge(sem[f"rsub{t}"], n + 1)
                else:
                    pe.wait_ge(sem[f"el{t}"], n + 1)
                mm(G[t][:, 0:wide], OT[p][:, t * 128:(t + 1) * 128], WS[:, lo:lo + wide], start=True, stop=True)\
                    .then_inc(sem[f"g{what}{t}"], 1)

            def hT(pe, n):
                pe.wait_ge(sem["h2"], n + 1)
                want(pe, "hz", n)
                for c in range(2):
                    for t in range(2):
                        k = (c * 2 + t) * 128
                        last = tr(XB[:, k:k + 128], H12[:, t * RW + c * 128:t * RW + c * 128 + 128], IDN[:])
                last.then_inc(sem["htp"], 1)

            def output(pe, n):
                pe.wait_ge(sem["ht"], n + 1)
                for t in range(2):
                    for c in range(2):
                        k = (c * 2 + t) * 128
                        last = mm(XB[:, t * C:(t + 1) * C], HT[:, k:k + 128], OW[:, c * C:(c + 1) * C],
                                  start=(c == 0), stop=(c == 1))
                last.then_inc(sem["ow"], 1)

            def hzT(pe, n):
                pe.wait_ge(sem["zz"], n + 1)
                for t in range(2):
                    last = tr(XB[:, 256 + t * 128:384 + t * 128], HZ[:, t * 128:(t + 1) * 128], IDN[:])
                last.then_inc(sem["ztp"], 1)

            def step(pe, s, pair, p, a, b1, b2):
                if b1:
                    slow(pe, s - 1, 1 - p, "rk", 0)
                    slow(pe, s - 1, 1 - p, "rk", 1)
                if a:
                    values(pe, s, pair, p)
                    scores(pe, s, p, 0)
                if b1:
                    slow(pe, s - 1, 1 - p, "qk", 0)
                if a:
                    scores(pe, s, p, 1)
                if b1:
                    slow(pe, s - 1, 1 - p, "qk", 1)
                if a:
                    probsT(pe, s, 0)
                if b1:
                    slow(pe, s - 1, 1 - p, "v", 0)
                if a:
                    attend(pe, s, 0)
                    probsT(pe, s, 1)
                if b1:
                    slow(pe, s - 1, 1 - p, "v", 1)
                if a:
                    attend(pe, s, 1)
                    ctxT(pe, s)
                    project(pe, s)
                if b2:
                    hT(pe, s - 2)
                    output(pe, s - 2)
                if a:
                    obsT(pe, s)
                if b2:
                    hzT(pe, s - 2)
            steps(pe, step)

            def feed(pe, g, p):
                want(pe, "fhe", g)
                mm(S[0][:], WI[:], HZT[0:C, bass.ds(g * 512, 512)], start=True, stop=True).then_inc(sem["fh"], 1)
                pe.wait_ge(sem["fhe"], g + 1)
                pe.wait_ge(sem["fsel0"], g + 1)
                want(pe, "fme0", g)
                fa = FA.rearrange("p (w n) -> p w n", w=8)
                for b in range(BLK):
                    last = mm(v3(S[1][:, b * 128:(b + 1) * 128], 16), WSEL[p][:, 0, b, 0:HID],
                              fa[:, :, b * 16:(b + 1) * 16], start=True, stop=True)
                last.then_inc(sem["fm0"], 1)
                pe.wait_ge(sem["fme0"], g + 1)
                pe.wait_ge(sem["fsel1"], g + 1)
                want(pe, "fme1", g)
                for b in range(BLK):
                    last = mm(TP[:, b * 128:(b + 1) * 128], WSEL[p][:, 1, b, 0:HID],
                              FB[:, b * 128:(b + 1) * 128], start=True, stop=True)
                last.then_inc(sem["fm1"], 1)
                pe.wait_ge(sem["fme1"], g + 1)
                want(pe, "foe", g)
                mm(CX[64:128, :], WO[:], FC, start=True, stop=True).then_inc(sem["fo"], 1)
            pe.wait_ge(sem["hz"], TILES)
            pe.wait_ge(sem["lde"], 112)
            feed(pe, 0, 0)
            feed(pe, 1, 1)
            with pe.Fori(1, GROUPS // 2) as g:
                feed(pe, g * 2, 0)
                feed(pe, g * 2 + 1, 1)


def _rotations():
    rot = np.zeros((128, 16, 2, 2, NH * 4), np.float32)
    half = HD // 2
    inv = 1.0 / 10000.0 ** (np.arange(0, half, 2, dtype=np.float32) / half)
    for v in range(16):
        for qk in range(2):
            scale = HD ** -0.5 if qk == 0 else 1.0
            for h in range(NH):
                for f in range(2):
                    a = np.float32(v % 8) * inv[f]
                    c, s = scale * np.cos(a), scale * np.sin(a)
                    src = qk * 64 + h * HD + (v // 8) * half + 2 * f
                    dst = h * 4 + 2 * f
                    rot[src, v, qk, :, dst] = c
                    rot[src + 1, v, qk, :, dst] = -s
                    rot[src, v, qk, :, dst + 1] = s
                    rot[src + 1, v, qk, :, dst + 1] = c
    return rot.reshape(128, 16 * 128)


def kernel(x, L0_tok_qkv_w, L0_tok_qkv_b, L0_tok_proj_w, L0_tok_proj_b, L0_attn_slow_W, L0_attn_out_W,
           L0_attn_ln_g, L0_attn_ln_b, L0_ffn_route_id, L0_ffn_Wi, L0_ffn_bi, L0_ffn_Wr, L0_ffn_br,
           L0_ffn_Ws, L0_ffn_bs, L0_ffn_Wo, L0_ffn_bo):
    import concourse.bacc as bacc
    from concourse.bass_utils import run_bass_kernel_spmd

    x, qkv_w, qkv_b, proj_w, proj_b, slow, outw, ln_g, ln_b, route, Wi, bi, Wr, br, Ws, bs, Wo, bo = (
        np.asarray(a) for a in (x, L0_tok_qkv_w, L0_tok_qkv_b, L0_tok_proj_w, L0_tok_proj_b, L0_attn_slow_W,
                                L0_attn_out_W, L0_attn_ln_g, L0_attn_ln_b, L0_ffn_route_id, L0_ffn_Wi,
                                L0_ffn_bi, L0_ffn_Wr, L0_ffn_br, L0_ffn_Ws, L0_ffn_bs, L0_ffn_Wo, L0_ffn_bo))
    x2 = x.reshape(B, 8, 8, 8, 8, C).transpose(0, 5, 1, 3, 2, 4).reshape(B * C, TOK)
    wv = qkv_w[128:192].reshape(4, 2, HD, C).transpose(3, 1, 0, 2).reshape(C, C)
    sw = slow.reshape(RH, 5 * RD + 2, C)
    fields = [sw[:, i * RD:(i + 1) * RD].reshape(RW, C) for i in range(5)]
    slowT = np.concatenate([fields[0], fields[1], fields[2], fields[4], fields[3], sw[:, 5 * RD], sw[:, 5 * RD + 1]]).T
    experts = np.concatenate([Wr.transpose(3, 0, 1, 2), br.transpose(2, 0, 1)[..., None]], -1).reshape(HID, -1)
    shared = np.concatenate([Ws[:, 0].transpose(2, 0, 1), bs[:, 0].T[..., None]], -1).reshape(HID, -1)
    p = np.arange(128)
    ins = dict(
        x2=x2, wqk=qkv_w[0:128], wv=wv, bqk=qkv_b[0:128, None], bv=qkv_b[128:192, None], projT=proj_w.T,
        projb=proj_b[None], rot=_rotations(),
        mask_img=((p[:, None] // 32) % 2 == np.arange(2)).astype(np.float32),
        mask_head=((p[:, None] % 32) // 4 == np.arange(NH)).astype(np.float32),
        ident_in=np.eye(128, dtype=np.float32), slowT=slowT, outT=outw.T, ln_g=ln_g[:, None], ln_b=ln_b[:, None],
        route=route[None], wiT=Wi.T, bi=bi[:, None], experts=experts, shared=shared, woT=Wo.T, bo=bo[:, None])
    nc = bacc.Bacc("TRN2", target_bir_lowering=False, num_devices=1)
    arrays, args = {}, []
    for name, a in ins.items():
        a = np.ascontiguousarray(a)
        arrays[f"in_{name}"] = a
        args.append(nc.dram_tensor(f"in_{name}", a.shape, mybir.dt.from_np(a.dtype), kind="ExternalInput").ap())
    out = nc.dram_tensor("out_0", (GROUPS, C, 512), F32, kind="ExternalOutput").ap()
    vit_tower(nc, *args, out)
    r = run_bass_kernel_spmd(nc, [arrays], core_ids=[0])
    y = r.results[0]["out_0"]
    y = y.reshape(B, 8, C, BLK, 8, 2, 8).transpose(0, 1, 3, 5, 4, 6, 2)
    return np.ascontiguousarray(y.reshape(B, TOK, C))
```

```python
from contextlib import ExitStack

import concourse.bass as bass
import numpy as np
from concourse import mybir

F32 = mybir.dt.float32
ALU = mybir.AluOpType
ACT = mybir.ActivationFunctionType
AX = mybir.AxisListType

B, HH, WW, C = 2, 64, 64, 64
WIN = 8
NTOK = WIN * WIN
NWIN = (HH // WIN) * (WW // WIN)
TILES = NWIN // 2
NH, HD = 8, 8
RH, RD = 8, 32
RW = RH * RD
HID, NE, NL = 128, 16, 2
EPS = 1e-5
TOK = HH * WW
GROUPS = 16
BLK = 4
EW = HID + 1
CQK, CV, CRK = 0, 2 * RW, 4 * RW
WCOLS = 5 * RW + 2 * RH
LAG = 4
LOOP_FROM = 6


def vit_tower(nc, x2, wqk, wv, bqk, bv, projT, projb, rot, mask_img, mask_head, ident_in,
              slowT, outT, ln_g, ln_b, route, wiT, bi, experts, shared, woT, bo, out):
    ctx = ExitStack()
    with ctx:
        def sb(name, shape):
            return ctx.enter_context(nc.sbuf_tensor(name, shape, F32))

        def bank(name):
            return ctx.enter_context(nc.psum_tensor(name, [128, 512], F32))

        IDN = sb("IDN", [128, 128])
        MIMG = sb("MIMG", [128, 2])
        MHEAD = sb("MHEAD", [128, NH])
        ROT = sb("ROT", [128, 16 * 128])
        WQK = sb("WQK", [128, C])
        BQK = sb("BQK", [128, 1])
        WROT = sb("WROT", [128, 16 * 128])
        QB = sb("QB", [128, 16])
        WV = sb("WV", [128, 2 * 64])
        PJ = sb("PJ", [128, 128])
        BV = sb("BV", [C, 1])
        BVB = sb("BVB", [C, 128])
        PROWB = sb("PROWB", [1, C])
        ONES = sb("ONES", [1, 128])
        PBIAS = sb("PBIAS", [128, 2 * C])
        WS = sb("WS", [C + 1, WCOLS])
        LNG = sb("LNG", [C, 1])
        LNB = sb("LNB", [C, 1])
        OW = sb("OW", [128, 2 * C])
        HALF = sb("HALF", [128, 4])
        NEG1 = sb("NEG1", [128, 1])
        ROUTE = ctx.enter_context(nc.sbuf_tensor("ROUTE", [1, 64], mybir.dt.int32))
        WI = sb("WI", [C, HID])
        BI = sb("BI", [HID, 1])
        EXP = sb("EXP", [128, NL * NE * EW])
        SHR = sb("SHR", [128, NL * EW])
        WO = sb("WO", [HID, C])
        BO = sb("BO", [128, 1])
        X2 = sb("X2", [128, TOK])
        Q2 = sb("Q2", [128, TOK])
        K2 = sb("K2", [128, TOK])
        HZT = sb("HZT", [128, B * TOK])
        XT = [sb(f"XT{p}", [128, 128]) for p in range(2)]
        QW = [sb(f"QW{p}", [128, 2 * 128]) for p in range(2)]
        KB = [[sb(f"KB{p}{w}", [128, 512]) for w in range(2)] for p in range(2)]
        NMX = [sb(f"NMX{w}", [128, NH]) for w in range(2)]
        SX = [sb(f"SX{w}", [128, 512]) for w in range(2)]
        PT = [sb(f"PT{w}", [128, 512]) for w in range(2)]
        VB = sb("VB", [128, 2 * 8 * 18])
        RDEN = sb("RDEN", [128, 16])
        CT = sb("CT", [128, 128])
        CTT = sb("CTT", [128, 128])
        H0 = sb("H0", [128, 128])
        ST1 = sb("ST1", [128, 12])
        MV1 = sb("MV1", [128, 4])
        PW1 = sb("PW1", [128, 4])
        RS1 = sb("RS1", [128, 4])
        NB1 = sb("NB1", [128, 4])
        RA = sb("RA", [128, 2])
        OH = sb("OH", [128, 128])
        RES = [sb(f"RES{p}", [128, 128]) for p in range(2)]
        OT = [sb(f"OT{p}", [C + 1, 256]) for p in range(2)]
        MR = sb("MR", [128, 2 * RH])
        BT = sb("BT", [128, 32])
        TH = sb("TH", [128, 32])
        BE = sb("BE", [128, 32])
        EQ = [sb(f"EQ{t}", [128, 512]) for t in range(2)]
        QK = sb("QK", [128, 2 * 512])
        RK = [sb(f"RK{p}", [128, 2 * RW]) for p in range(2)]
        V = [sb(f"V{p}", [128, 2 * 512]) for p in range(2)]
        PR = sb("PR", [128, 5 * RW])
        SM = sb("SM", [128, 48])
        RC = sb("RC", [128, 48])
        DT = sb("DT", [128, 40])
        NM = sb("NM", [128, 40])
        CC = [sb(f"CC{p}", [128, 16]) for p in range(2)]
        CF = [sb(f"CF{p}", [128, 32]) for p in range(2)]
        UU = [sb(f"UU{p}", [128, 16]) for p in range(2)]
        GG = [sb(f"GG{p}", [128, 8]) for p in range(2)]
        TA = sb("TA", [128, 8])
        HM = sb("HM", [128, 512])
        H12 = sb("H12", [128, 2 * RW])
        MH = sb("MH", [128, RH])
        QX = sb("QX", [128, RW])
        PQ = sb("PQ", [128, 3 * RW])
        DQ = sb("DQ", [128, 24])
        RQ = sb("RQ", [128, 8])
        TU = sb("TU", [128, 16])
        TB = sb("TB", [128, 8])
        HM2 = sb("HM2", [128, 1024])
        A1 = sb("A1", [128, 512])
        HT = sb("HT", [128, 512])
        HZ = sb("HZ", [128, 256])
        ST2 = sb("ST2", [128, 12])
        MV2 = sb("MV2", [128, 4])
        PW2 = sb("PW2", [128, 2])
        RS2 = sb("RS2", [128, 2])
        NB2 = sb("NB2", [128, 2])
        WSEL = [X2[:, p * 2048:p * 2048 + 8 * EW].rearrange("p (l b e) -> p l b e", l=NL, b=BLK)
                for p in range(2)]
        FA = [Q2[:, p * 512:(p + 1) * 512] for p in range(2)]
        FB = [Q2[:, 1024 + p * 512:1536 + p * 512] for p in range(2)]
        FC = [Q2[:, 2048 + p * 512:2560 + p * 512] for p in range(2)]
        FO = [K2[64:128, p * 512:(p + 1) * 512] for p in range(2)]

        S = [bank("S0"), bank("S1")]
        TP = bank("TP")
        CX = bank("CX")
        XA = bank("XA")
        XB = bank("XB")
        G = [bank("G0"), bank("G1")]
        PH, P0, P1, PO = S, G, [TP, CX], [XA, XB]

        names = """ldw ldx ldp lds lde stw zero zro1 wr wre qbm qbe qkp0 qkp1 qke0 qke1 bvb pbm pbe wsb wss
            shi setd xt0 xt1 qw kb0 kb1 vp vb sc0 sc1 mx0 mx1 sb0 sb1 ex0 ex1 tp0 tp1 pt0 pt1 pv0 pv1 rd cx ctp ctt pj h0
            bs1 bv1 pw1 rs1 nb1 oh res otp ot
            grk0 grk1 gqk0 gqk1 gv0 gv1 mr rsub0 rsub1 rk0 rk1 th eq0 eq1 el0 el1 vv0 vv1 pra prr sq sr rp rc be n1 n2
            n3 n4 cc cf0 hm h1 mh qx qr pq dq rq t1 t2 cf1 cft hm2 a1 h2 htp ht ow yy bs2 bv2 pw2 rs2 nb2 zz ztp hz
            fsel0 fsel1 fh fhe fm0 fme0 fm1 fme1 fo foe fst0 fst1""".split()
        sem = {n: ctx.enter_context(nc.semaphore("s_" + n)) for n in names}

        def want(eng, name, n):
            if not isinstance(n, int) or n > 0:
                eng.wait_ge(sem[name], n)

        def v3(ap, b):
            return ap.rearrange("p (a b) -> p a b", b=b)

        def over(ap, k):
            return ap.unsqueeze(2).to_broadcast([ap.shape[0], ap.shape[1], k])

        def steps(step, eng, count=TILES, lag=LAG, loop_from=LOOP_FROM):
            for s in range(loop_from):
                step(s, s % 2, s // 2, lambda k, s=s: 0 <= s - k < count)
            with eng.Fori(loop_from // 2, count // 2) as i:
                for p in range(2):
                    step(i * 2 + p, p, i, lambda k: True)
            for s in range(count, count + lag):
                step(s, s % 2, s // 2, lambda k, s=s: 0 <= s - k < count)

        block = ctx.enter_context(nc.Block())

        @block.sync
        def _(sp):
            sp.dma_start(WQK[:], wqk).then_inc(sem["ldw"], 16)
            sp.dma_start(BQK[:], bqk).then_inc(sem["ldw"], 16)
            sp.dma_start(ROT[:], rot).then_inc(sem["ldw"], 16)
            sp.dma_start(X2[:], x2).then_inc(sem["ldx"], 16)
            sp.dma_start(MIMG[:], mask_img).then_inc(sem["ldp"], 16)
            sp.dma_start(MHEAD[:], mask_head).then_inc(sem["ldp"], 16)
            sp.dma_start(IDN[:], ident_in).then_inc(sem["ldp"], 16)
            sp.wait_ge(sem["zero"], 1)
            for t in range(2):
                for e in range(2):
                    sp.dma_start(WV[64 * t:64 * t + 64, e * 64 + t * 32:e * 64 + t * 32 + 32],
                                 wv[:, e * 32:(e + 1) * 32]).then_inc(sem["lds"], 16)
                sp.dma_start(PJ[64 * t:64 * t + 64, t * C:(t + 1) * C], projT).then_inc(sem["lds"], 16)
            sp.dma_start(BV[:], bv).then_inc(sem["lds"], 16)
            sp.dma_start(PROWB[:], projb).then_inc(sem["lds"], 16)
            sp.dma_start(WS[0:C, :], slowT).then_inc(sem["lds"], 16)
            sp.dma_start(LNG[:], ln_g).then_inc(sem["lds"], 16)
            sp.dma_start(LNB[:], ln_b).then_inc(sem["lds"], 16)
            for c in range(2):
                sp.dma_start(OW[:, c * C:(c + 1) * C], outT[c * 128:(c + 1) * 128, :]).then_inc(sem["lds"], 16)
            sp.dma_start(WI[:], wiT).then_inc(sem["lde"], 16)
            sp.dma_start(BI[:], bi).then_inc(sem["lde"], 16)
            sp.dma_start(WO[:], woT).then_inc(sem["lde"], 16)
            sp.dma_start(BO[64:128, :], bo).then_inc(sem["lde"], 16)
            sp.dma_start(ROUTE[:], route).then_inc(sem["lde"], 16)
            sp.dma_start(SHR[:], shared).then_inc(sem["lde"], 16)
            sp.dma_start(EXP[:], experts).then_inc(sem["lde"], 16)

            def load_tile(sp, n, p):
                want(sp, "vp", n - 1)
                sp.dma_start(XT[p][:], x2[:, bass.ds(n * 128, 128)]).then_inc(sem[f"xt{p}"], 16)
            load_tile(sp, 0, 0)
            load_tile(sp, 1, 1)
            with sp.Fori(1, TILES // 2) as i:
                load_tile(sp, i * 2, 0)
                load_tile(sp, i * 2 + 1, 1)
            sp.wait_ge(sem["foe"], 1)
            sp.dma_start(out[0], FO[0]).then_inc(sem["fst0"], 16)
            sp.wait_ge(sem["foe"], 2)
            sp.dma_start(out[1], FO[1]).then_inc(sem["fst1"], 16)
            with sp.Fori(1, GROUPS // 2) as g:
                for p in range(2):
                    sp.wait_ge(sem["foe"], g * 2 + (p + 1))
                    sp.dma_start(out[bass.ds(g * 2 + p, 1)].rearrange("a c n -> (a c) n"), FO[p]).then_inc(sem[f"fst{p}"], 16)
            sp.wait_ge(sem["fst0"], 8 * GROUPS)
            sp.wait_ge(sem["fst1"], 8 * GROUPS)

        @block.gpsimd
        def _(pool):
            pool.wait_ge(sem["ldp"], 48)
            pool.wait_ge(sem["zro1"], 3)

            def prepare(pool, n, p):
                want(pool, "sc1", n - 1)
                nc.gpsimd.tensor_tensor(
                    QW[p][:].rearrange("p (w t q) -> p w t q", w=2, t=2),
                    Q2[:, bass.ds(n * 128, 128)].rearrange("p (w q) -> p w q", w=2).unsqueeze(2)
                    .to_broadcast([128, 2, 2, NTOK]),
                    MIMG[:].unsqueeze(1).unsqueeze(3).to_broadcast([128, 2, 2, NTOK]),
                    ALU.mult).then_inc(sem["qw"], 1)
                for w in range(2):
                    nc.gpsimd.tensor_tensor(
                        v3(KB[p][w][:], NTOK),
                        K2[:, bass.ds(n * 128 + w * 64, 64)].unsqueeze(1).to_broadcast([128, NH, NTOK]),
                        over(MHEAD[:], NTOK), ALU.mult).then_inc(sem[f"kb{w}"], 1)

            def rsqrt1(pool, n, p):
                pool.wait_ge(sem["pw1"], n + 1)
                want(pool, "oh", n)
                want(pool, "nb1", n)
                nc.gpsimd.tensor_tensor(RS1[:], PW1[:], HALF[:], ALU.pow).then_inc(sem["rs1"], 1)

            def products(pool, n, p):
                qk = QK[:]
                want(pool, "rp", n)
                pool.wait_ge(sem["el0"], n + 1)
                nc.gpsimd.tensor_tensor(PR[:, 2 * RW:3 * RW], qk[:, 0:RW], qk[:, RW:2 * RW], ALU.mult)
                pool.wait_ge(sem["el1"], n + 1)
                nc.gpsimd.tensor_tensor(v3(PR[:, 0:2 * RW], RW), v3(qk[:, 2 * RW:4 * RW], RW),
                                        qk[:, RW:2 * RW].unsqueeze(1).to_broadcast([128, 2, RW]), ALU.mult)
                nc.gpsimd.tensor_tensor(PR[:, 3 * RW:4 * RW], qk[:, 2 * RW:3 * RW], qk[:, 3 * RW:4 * RW],
                                        ALU.mult).then_inc(sem["pra"], 1)

            def key_product(pool, n, p):
                pool.wait_ge(sem["rk0"], n + 1)
                pool.wait_ge(sem["rk1"], n + 1)
                want(pool, "rp", n)
                nc.gpsimd.tensor_tensor(PR[:, 4 * RW:5 * RW], RK[p][:, 0:RW], RK[p][:, RW:2 * RW],
                                        ALU.mult).then_inc(sem["prr"], 1)

            def first_state(pool, n, p):
                pool.wait_ge(sem["cc"], n + 1)
                pool.wait_ge(sem["vv0"], n + 1)
                want(pool, "h1", n)
                nc.gpsimd.tensor_tensor(v3(HM[:], RD), v3(V[p][:, 0:512], RD), over(CC[p][:], RD),
                                        ALU.mult).then_inc(sem["hm"], 1)

            def state_sum(pool, n, p):
                pool.wait_ge(sem["hm"], n + 1)
                want(pool, "htp", n)
                nc.gpsimd.tensor_tensor(H12[:, 0:RW], HM[:, 0:RW], HM[:, RW:2 * RW], ALU.add).then_inc(sem["h1"], 1)

            def query_products(pool, n, p):
                pool.wait_ge(sem["qr"], n + 1)
                nc.gpsimd.tensor_tensor(v3(PQ[:, RW:3 * RW], RW), v3(RK[p][:], RW),
                                        PQ[:, 0:RW].unsqueeze(1).to_broadcast([128, 2, RW]),
                                        ALU.mult).then_inc(sem["pq"], 1)

            def second_state(pool, n, p):
                pool.wait_ge(sem["cf1"], n + 1)
                pool.wait_ge(sem["vv1"], n + 1)
                want(pool, "a1", n)
                nc.gpsimd.tensor_tensor(v3(HM2[:], RD), v3(V[p][:], RD), over(CF[p][:], RD),
                                        ALU.mult).then_inc(sem["hm2"], 1)

            def rsqrt2(pool, n, p):
                pool.wait_ge(sem["pw2"], n + 1)
                want(pool, "zz", n)
                nc.gpsimd.tensor_tensor(RS2[:], PW2[:], HALF[:, 0:2], ALU.pow).then_inc(sem["rs2"], 1)

            pool.wait_ge(sem["qke0"], 16)
            pool.wait_ge(sem["qke1"], 16)
            def step(s, sp, half, live):
                if live(0):
                    prepare(pool, s, sp)
                if live(3):
                    first_state(pool, s - 3, 1 - sp)
                    state_sum(pool, s - 3, 1 - sp)
                if live(2):
                    key_product(pool, s - 2, sp)
                    products(pool, s - 2, sp)
                if live(3):
                    query_products(pool, s - 3, 1 - sp)
                if live(1):
                    rsqrt1(pool, s - 1, 1 - sp)
                if live(4):
                    rsqrt2(pool, s - 4, sp)
                if live(3):
                    second_state(pool, s - 3, 1 - sp)
            steps(step, pool)

            pool.wait_ge(sem["lde"], 112)
            pool.wait_ge(sem["shi"], 1)
            pool.wait_ge(sem["ztp"], TILES)

            def select(pool, g, p):
                want(pool, "fme1", g - 1)
                for b in range(BLK):
                    e = pool.value_load(ROUTE[0:1, bass.ds(g * BLK + b, 1)], min_val=0, max_val=NE - 1)
                    last = nc.gpsimd.tensor_tensor(WSEL[p][:, 1, b, :], EXP[:, bass.ds(e * EW + NE * EW, EW)],
                                                   SHR[:, EW:2 * EW], ALU.add)
                last.then_inc(sem["fsel1"], 1)
            select(pool, 0, 0)
            select(pool, 1, 1)
            with pool.Fori(1, GROUPS // 2) as g:
                select(pool, g * 2, 0)
                select(pool, g * 2 + 1, 1)

        @block.scalar
        def _(act):
            a_ = nc.scalar.activation
            wrot = WROT[:].rearrange("p (v q t d) -> p v q t d", v=16, q=2, t=2)
            act.wait_ge(sem["zro1"], 1)
            for t in range(2):
                act.wait_ge(sem["wr"], t + 1)
                for half in range(2):
                    for qk in range(2):
                        last = a_(wrot[64 * t:64 * t + 64, half * 8:(half + 1) * 8, qk, t, :],
                                  G[half][64 * t:64 * t + 64, :].rearrange("p (v q d) -> p v q d", v=8, q=2)[:, :, qk, :],
                                  ACT.Copy)
                last.then_inc(sem["wre"], 1)
            act.wait_ge(sem["qbm"], 1)
            a_(QB[:], XA[:, 0:16], ACT.Copy).then_inc(sem["qbe"], 1)
            act.wait_ge(sem["qbe"], 1)
            for v in range(0, 16, 2):
                act.wait_ge(sem["qkp0"], v // 2 + 1)
                half, pos = v // 8, v % 8
                for qk, dst in ((0, Q2), (1, K2)):
                    d = dst[64 * half:64 * half + 64, :].rearrange("p (w r c) -> p w r c", r=8, c=8)
                    d = d[:, :, pos, :] if half == 0 else d[:, :, :, pos]
                    a_(d, v3(G[0][64 * qk:64 * qk + 64, :], 8), ACT.Identity,
                       bias=QB[64 * qk:64 * qk + 64, v:v + 1]).then_inc(sem["qke0"], 1)
            act.wait_ge(sem["pbm"], 1)
            for t in range(2):
                last = a_(PBIAS[:, t * C:(t + 1) * C], XB[:, 0:C], ACT.Copy)
            last.then_inc(sem["pbe"], 1)
            act.wait_ge(sem["zro1"], 4)

            vb = VB[:].rearrange("p (a c) -> p a c", c=18)

            def values(act, n, p):
                act.wait_ge(sem["vp"], n + 1)
                want(act, "pv1", n)
                for e in range(2):
                    last = a_(vb[64 * e:64 * e + 64, :, 9 * e:9 * e + 8],
                              v3(XA[64 * e:64 * e + 64, 0:128], 8), ACT.Copy)
                last.then_inc(sem["vb"], 1)

            def exps(act, n, p, w):
                act.wait_ge(sem[f"mx{w}"], n + 1)
                want(act, f"tp{w}", n)
                for h in range(NH):
                    last = a_(SX[w][:, h * NTOK:(h + 1) * NTOK], S[w][:, h * NTOK:(h + 1) * NTOK], ACT.Exp,
                              bias=NMX[w][:, h:h + 1])
                last.then_inc(sem[f"ex{w}"], 1)

            def probsT(act, n, p, w):
                act.wait_ge(sem[f"tp{w}"], n + 1)
                want(act, f"pv{w}", n)
                a_(PT[w][:], TP[:], ACT.Copy).then_inc(sem[f"pt{w}"], 1)

            def ctxT(act, n, p):
                act.wait_ge(sem["ctp"], n + 1)
                want(act, "pj", n)
                a_(CTT[:], XA[:, 128:256], ACT.Copy).then_inc(sem["ctt"], 1)

            def normed1(act, n, p):
                act.wait_ge(sem["nb1"], n + 1)
                want(act, "otp", n)
                for t in range(2):
                    last = a_(OH[:, 64 * t:64 * t + 64], H0[:, 64 * t:64 * t + 64], ACT.Identity,
                              scale=RS1[:, 2 * t:2 * t + 1], bias=NB1[:, 2 * t:2 * t + 1])
                last.then_inc(sem["oh"], 1)

            def residual(act, n, p):
                act.wait_ge(sem["nb1"], n + 1)
                want(act, "yy", n - 1)
                for t in range(2):
                    last = a_(RES[p][:, 64 * t:64 * t + 64], H0[:, 64 * t:64 * t + 64], ACT.Identity,
                              scale=RA[:, t:t + 1], bias=NB1[:, 2 * t + 1:2 * t + 2])
                last.then_inc(sem["res"], 1)

            def normed2(act, n, p):
                act.wait_ge(sem["nb2"], n + 1)
                hz = HZ[:].rearrange("p (t k c) -> p t k c", t=2, k=2)
                for t in range(2):
                    last = a_(hz[:, t, 0, :], hz[:, t, 1, :], ACT.Identity, scale=RS2[:, t:t + 1],
                              bias=NB2[:, t:t + 1])
                last.then_inc(sem["zz"], 1)

            def obsT(act, n, p):
                act.wait_ge(sem["otp"], n + 1)
                want(act, "gv1", n - 1)
                a_(OT[p][0:C, :], XA[0:C, 0:256], ACT.Copy).then_inc(sem["ot"], 1)

            def rk_exp(act, n, p, t):
                act.wait_ge(sem[f"rsub{t}"], n + 1)
                a_(RK[p][:, t * RW:(t + 1) * RW], RK[p][:, t * RW:(t + 1) * RW], ACT.Exp).then_inc(sem[f"rk{t}"], 1)

            def gates(act, n, p):
                act.wait_ge(sem["rsub1"], n + 1)
                want(act, "be", n)
                a_(TH[:], BT[:], ACT.Tanh, scale=0.5).then_inc(sem["th"], 1)

            def qk_exp(act, n, p, t):
                act.wait_ge(sem[f"gqk{t}"], n + 1)
                want(act, f"el{t}", n)
                a_(EQ[t][:], G[t][:], ACT.Exp, bias=NEG1[:, 0:1]).then_inc(sem[f"eq{t}"], 1)

            def v_copy(act, n, p, t):
                act.wait_ge(sem[f"gv{t}"], n + 1)
                want(act, "hm2", n - 1)
                a_(V[p][:, t * 512:(t + 1) * 512], G[t][:], ACT.Copy).then_inc(sem[f"vv{t}"], 1)

            def query_exp(act, n, p):
                act.wait_ge(sem["qx"], n + 1)
                want(act, "dq", n)
                want(act, "pq", n)
                a_(PQ[:, 0:RW], QX[:], ACT.Exp).then_inc(sem["qr"], 1)

            def hT(act, n, p):
                act.wait_ge(sem["htp"], n + 1)
                want(act, "ow", n)
                a_(HT[:], XB[:], ACT.Copy).then_inc(sem["ht"], 1)

            def hzT(act, n, p):
                act.wait_ge(sem["ztp"], n + 1)
                a_(HZT[:].rearrange("p (t c) -> p t c", t=2)[:, :, bass.ds(n * 128, 128)],
                   v3(XB[:, 256:512], 128), ACT.Copy).then_inc(sem["hz"], 1)

            act.wait_ge(sem["ldp"], 48)
            def step(s, sp, half, live):
                if live(2):
                    residual(act, s - 2, sp)
                if live(1):
                    ctxT(act, s - 1, 1 - sp)
                if live(3):
                    query_exp(act, s - 3, 1 - sp)
                if live(0):
                    exps(act, s, sp, 0)
                if live(2):
                    v_copy(act, s - 2, sp, 0)
                    v_copy(act, s - 2, sp, 1)
                if live(1):
                    normed1(act, s - 1, 1 - sp)
                if live(0):
                    probsT(act, s, sp, 0)
                if live(1):
                    obsT(act, s - 1, 1 - sp)
                if live(0):
                    exps(act, s, sp, 1)
                    values(act, s, sp)
                if live(4):
                    normed2(act, s - 4, sp)
                if live(0):
                    probsT(act, s, sp, 1)
                if live(4):
                    hzT(act, s - 4, sp)
                if live(1):
                    gates(act, s - 1, 1 - sp)
                    rk_exp(act, s - 1, 1 - sp, 0)
                    rk_exp(act, s - 1, 1 - sp, 1)
                    qk_exp(act, s - 1, 1 - sp, 0)
                    qk_exp(act, s - 1, 1 - sp, 1)
                if live(3):
                    hT(act, s - 3, 1 - sp)
            steps(step, act)

            def relu0(act, g, p):
                act.wait_ge(sem["fh"], g + 1)
                want(act, "fm0", g - 1)
                a_(FA[p], PH[p][:], ACT.Relu, bias=BI[:, 0:1]).then_inc(sem["fhe"], 1)

            def relu1(act, g, p):
                act.wait_ge(sem["fm0"], g + 1)
                want(act, "fm1", g - 1)
                for b in range(BLK):
                    last = a_(FB[p][:, b * 128:(b + 1) * 128], P0[p][:, b * 128:(b + 1) * 128], ACT.Relu,
                              bias=WSEL[p][:, 0, b, HID:HID + 1])
                last.then_inc(sem["fme0"], 1)

            def relu2(act, g, p):
                act.wait_ge(sem["fm1"], g + 1)
                want(act, "fo", g - 1)
                for b in range(BLK):
                    last = a_(FC[p][:, b * 128:(b + 1) * 128], P1[p][:, b * 128:(b + 1) * 128], ACT.Relu,
                              bias=WSEL[p][:, 1, b, HID:HID + 1])
                last.then_inc(sem["fme1"], 1)

            def feed(s, sp, half, live):
                if live(0):
                    relu0(act, s, sp)
                if live(1):
                    relu1(act, s - 1, 1 - sp)
                if live(2):
                    relu2(act, s - 2, sp)
            steps(feed, act, GROUPS, 3, 6)

        @block.vector
        def _(dve):
            v_ = nc.vector
            v_.memset(WROT[:], 0.0).then_inc(sem["zro1"], 1)
            v_.memset(WV[:], 0.0)
            v_.memset(PJ[:], 0.0)
            v_.memset(ONES[:], 1.0).then_inc(sem["zero"], 1)
            v_.memset(VB[:], 0.0).then_inc(sem["zro1"], 1)
            v_.memset(HALF[:], -0.5)
            v_.memset(NEG1[:], -1.0)
            v_.memset(OT[0][C:C + 1, :], 1.0)
            v_.memset(OT[1][C:C + 1, :], 1.0).then_inc(sem["zro1"], 1)
            dve.wait_ge(sem["zro1"], 3)
            ones = VB[:].rearrange("p (a c) -> p a c", c=18)
            v_.memset(ones[0:64, :, 8:9], 1.0)
            v_.memset(ones[64:128, :, 17:18], 1.0).then_inc(sem["zro1"], 1)
            dve.wait_ge(sem["lds"], 16 * 13)
            v_.memset(BVB[:], 1.0).then_inc(sem["setd"], 1)
            dve.wait_ge(sem["setd"], 1)
            v_.tensor_scalar(BVB[:], BVB[:], BV[:, 0:1], None, ALU.mult).then_inc(sem["bvb"], 1)
            dve.wait_ge(sem["qbe"], 1)
            for v in range(1, 16, 2):
                dve.wait_ge(sem["qkp1"], v // 2 + 1)
                half, pos = v // 8, v % 8
                for qk, dst in ((0, Q2), (1, K2)):
                    d = dst[64 * half:64 * half + 64, :].rearrange("p (w r c) -> p w r c", r=8, c=8)
                    d = d[:, :, pos, :] if half == 0 else d[:, :, :, pos]
                    v_.tensor_scalar(d, v3(G[1][64 * qk:64 * qk + 64, :], 8),
                                     QB[64 * qk:64 * qk + 64, v:v + 1], None, ALU.add).then_inc(sem["qke1"], 1)
            dve.wait_ge(sem["wsb"], 3)
            v_.tensor_scalar(WS[C:C + 1, 0:512], S[0][C:C + 1, 0:512], 1.0, None, ALU.add)
            v_.tensor_copy(WS[C:C + 1, 512:1024], S[1][C:C + 1, 0:512])
            v_.tensor_copy(WS[C:C + 1, 1024:WCOLS], TP[C:C + 1, 0:WCOLS - 1024])
            v_.tensor_scalar(WS[0:C, :], WS[0:C, :], LNG[:, 0:1], None, ALU.mult).then_inc(sem["wss"], 1)
            dve.wait_ge(sem["lde"], 112)
            dve.wait_ge(sem["ldp"], 48)
            for l in range(NL):
                last = v_.tensor_tensor(SHR[:, l * EW:l * EW + HID], SHR[:, l * EW:l * EW + HID], IDN[:], ALU.add)
            last.then_inc(sem["shi"], 1)
            dve.wait_ge(sem["pbe"], 1)

            def rowmax(dve, n, p, w):
                dve.wait_ge(sem[f"sc{w}"], n + 1)
                v_.tensor_reduce(NMX[w][:], v3(S[w][:], NTOK), AX.X, ALU.max, negate=True).then_inc(sem[f"mx{w}"], 1)

            cx = CX[:, 0:144].rearrange("p (a c) -> p a c", c=9)

            def denominators(dve, n, p):
                dve.wait_ge(sem["pv1"], n + 1)
                v_.reciprocal(RDEN[:], cx[:, :, 8]).then_inc(sem["rd"], 1)

            def ctx_norm(dve, n, p):
                dve.wait_ge(sem["rd"], n + 1)
                want(dve, "ctp", n)
                v_.tensor_tensor(v3(CT[:], 8), cx[:, :, 0:8], over(RDEN[:], 8), ALU.mult).then_inc(sem["cx"], 1)

            def hidden0(dve, n, p):
                dve.wait_ge(sem["pj"], n + 1)
                want(dve, "oh", n)
                want(dve, "res", n)
                v_.tensor_tensor(H0[:], XA[:, 256:384], PBIAS[:], ALU.add).then_inc(sem["h0"], 1)

            def stats1(dve, n, p):
                dve.wait_ge(sem["h0"], n + 1)
                for t in range(2):
                    last = v_.bn_stats(ST1[:, 6 * t:6 * t + 6], H0[:, 64 * t:64 * t + 64])
                last.then_inc(sem["bs1"], 1)

            def mean_var1(dve, n, p):
                dve.wait_ge(sem["pbe"], 1)
                dve.wait_ge(sem["bs1"], n + 1)
                for t in range(2):
                    last = v_.bn_aggr(MV1[:, 2 * t:2 * t + 2], ST1[:, 6 * t:6 * t + 6])
                last.then_inc(sem["bv1"], 1)

            def radicand1(dve, n, p):
                dve.wait_ge(sem["bv1"], n + 1)
                want(dve, "rs1", n)
                mv, pw = v3(MV1[:], 2), v3(PW1[:], 2)
                v_.tensor_scalar(pw[:, :, 0], mv[:, :, 1], 1.0 + EPS, EPS * EPS, ALU.mult, ALU.add)
                v_.tensor_scalar(pw[:, :, 1], mv[:, :, 1], EPS, None, ALU.add).then_inc(sem["pw1"], 1)

            def shift1(dve, n, p):
                dve.wait_ge(sem["rs1"], n + 1)
                want(dve, "oh", n)
                want(dve, "res", n)
                mv, rs = v3(MV1[:], 2), v3(RS1[:], 2)
                v_.tensor_scalar(RA[:], rs[:, :, 1], 1.0, None, ALU.add)
                v_.scalar_tensor_tensor(v3(NB1[:], 2), mv[:, :, 0:1].to_broadcast([128, 2, 2]), -1.0, rs,
                                        ALU.mult, ALU.mult).then_inc(sem["nb1"], 1)

            def rk_max(dve, n, p):
                for t in range(2):
                    dve.wait_ge(sem[f"grk{t}"], n + 1)
                    last = v_.tensor_reduce(MR[:, t * RH:(t + 1) * RH], v3(G[t][:, 0:RW], RD), AX.X, ALU.max)
                last.then_inc(sem["mr"], 1)

            def rk_sub(dve, n, p):
                dve.wait_ge(sem["mr"], n + 1)
                want(dve, "th", n)
                want(dve, "pq", n - 1)
                for t in range(2):
                    v_.tensor_copy(BT[:, t * 16:(t + 1) * 16], G[t][:, RW:RW + 16])
                    v_.tensor_tensor(v3(RK[p][:, t * RW:(t + 1) * RW], RD), v3(G[t][:, 0:RW], RD),
                                     over(MR[:, t * RH:(t + 1) * RH], RD), ALU.subtract).then_inc(sem[f"rsub{t}"], 1)

            def elu(dve, n, p, t):
                dve.wait_ge(sem[f"eq{t}"], n + 1)
                want(dve, "pra", n)
                v_.scalar_tensor_tensor(QK[:, t * 512:(t + 1) * 512], G[t][:], 1.0, EQ[t][:],
                                        ALU.max, ALU.min).then_inc(sem[f"el{t}"], 1)

            def qk_sums(dve, n, p):
                dve.wait_ge(sem["el0"], n + 1)
                dve.wait_ge(sem["el1"], n + 1)
                want(dve, "rc", n)
                v_.tensor_reduce(SM[:, 0:32], v3(QK[:], RD), AX.X, ALU.add).then_inc(sem["sq"], 1)

            def rk_sums(dve, n, p):
                dve.wait_ge(sem["rk0"], n + 1)
                dve.wait_ge(sem["rk1"], n + 1)
                want(dve, "rc", n)
                v_.tensor_reduce(SM[:, 32:48], v3(RK[p][:], RD), AX.X, ALU.add).then_inc(sem["sr"], 1)

            def strengths(dve, n, p):
                dve.wait_ge(sem["th"], n + 1)
                want(dve, "n3", n)
                v_.tensor_scalar(BE[:], TH[:], 0.5, 0.5, ALU.mult, ALU.add).then_inc(sem["be"], 1)

            def inverses(dve, n, p):
                dve.wait_ge(sem["sq"], n + 1)
                dve.wait_ge(sem["sr"], n + 1)
                want(dve, "n3", n)
                v_.reciprocal(RC[:], SM[:]).then_inc(sem["rc"], 1)

            def dots(dve, n, p):
                dve.wait_ge(sem["pra"], n + 1)
                dve.wait_ge(sem["prr"], n + 1)
                want(dve, "n1", n)
                v_.tensor_reduce(DT[:], v3(PR[:], RD), AX.X, ALU.add).then_inc(sem["rp"], 1)

            be = BE[:].rearrange("p (t k h) -> p t k h", t=2, k=2)
            rc, dt, nm = v3(RC[:], 8), v3(DT[:], 8), v3(NM[:], 8)

            def coef(p):
                return CF[p][:].rearrange("p (t k h) -> p t k h", t=2, k=2)

            def coefs1(dve, n, p):
                dve.wait_ge(sem["rp"], n + 1)
                dve.wait_ge(sem["rc"], n + 1)
                dve.wait_ge(sem["be"], n + 1)
                want(dve, "hm2", n - 1)
                v_.tensor_tensor(nm[:, 0:2], dt[:, 0:2], rc[:, 2:4], ALU.mult)
                v_.tensor_tensor(nm[:, 2:4], dt[:, 2:4], rc[:, 0:3:2], ALU.mult)
                v_.tensor_tensor(nm[:, 4], dt[:, 4], rc[:, 4], ALU.mult).then_inc(sem["n1"], 1)
                v_.tensor_tensor(v3(UU[p][:], 8), be[:, :, 1, :], rc[:, 4:6], ALU.mult)

            def coefs2(dve, n, p):
                dve.wait_ge(sem["n1"], n + 1)
                v_.tensor_tensor(nm[:, 0:3], nm[:, 0:3], rc[:, 1:2].to_broadcast([128, 3, 8]), ALU.mult)
                v_.tensor_tensor(nm[:, 3], nm[:, 3], rc[:, 3], ALU.mult)
                v_.tensor_tensor(nm[:, 4], nm[:, 4], rc[:, 5], ALU.mult).then_inc(sem["n2"], 1)
                v_.tensor_scalar(CC[p][:, 8:16], be[:, 0, 1, :], 1.0 / RD, None, ALU.mult)

            def coefs3(dve, n, p):
                dve.wait_ge(sem["n2"], n + 1)
                v_.tensor_tensor(nm[:, 0:3], nm[:, 0:3], be[:, 0:1, 0, :].to_broadcast([128, 3, 8]), ALU.mult)
                v_.tensor_tensor(coef(p)[:, 1, 0, :], nm[:, 3], be[:, 1, 0, :], ALU.mult)
                v_.tensor_tensor(GG[p][:], nm[:, 4], be[:, 0, 1, :], ALU.mult).then_inc(sem["n3"], 1)

            def coefs4(dve, n, p):
                dve.wait_ge(sem["n3"], n + 1)
                v_.tensor_copy(CC[p][:, 0:8], nm[:, 2]).then_inc(sem["cc"], 1)
                v_.tensor_tensor(TA[:], coef(p)[:, 1, 0, :], nm[:, 1], ALU.mult).then_inc(sem["n4"], 1)

            def coefs5(dve, n, p):
                dve.wait_ge(sem["n4"], n + 1)
                v_.tensor_tensor(coef(p)[:, 0, 0, :], nm[:, 0], TA[:], ALU.subtract).then_inc(sem["cf0"], 1)

            def h_max(dve, n, p):
                dve.wait_ge(sem["h1"], n + 1)
                v_.tensor_reduce(MH[:], v3(H12[:, 0:RW], RD), AX.X, ALU.max).then_inc(sem["mh"], 1)

            def h_query(dve, n, p):
                dve.wait_ge(sem["mh"], n + 1)
                want(dve, "qr", n)
                v_.tensor_tensor(v3(QX[:], RD), v3(H12[:, 0:RW], RD), over(MH[:], RD),
                                 ALU.subtract).then_inc(sem["qx"], 1)

            def query_dots(dve, n, p):
                dve.wait_ge(sem["pq"], n + 1)
                want(dve, "rq", n)
                v_.tensor_reduce(DQ[:], v3(PQ[:], RD), AX.X, ALU.add).then_inc(sem["dq"], 1)

            def query1(dve, n, p):
                dve.wait_ge(sem["dq"], n + 1)
                v_.reciprocal(RQ[:], DQ[:, 0:8])
                v_.tensor_tensor(TU[:], UU[p][:], DQ[:, 8:24], ALU.mult).then_inc(sem["rq"], 1)

            def query2(dve, n, p):
                dve.wait_ge(sem["rq"], n + 1)
                v_.tensor_tensor(v3(TU[:], 8), v3(TU[:], 8), RQ[:].unsqueeze(1).to_broadcast([128, 2, 8]),
                                 ALU.mult).then_inc(sem["t1"], 1)

            def query3(dve, n, p):
                dve.wait_ge(sem["t1"], n + 1)
                dve.wait_ge(sem["cf0"], n + 1)
                v_.tensor_tensor(TB[:], TU[:, 8:16], GG[p][:], ALU.mult).then_inc(sem["t2"], 1)
                v_.tensor_copy(coef(p)[:, 1, 1, :], TU[:, 8:16])

            def query4(dve, n, p):
                dve.wait_ge(sem["t2"], n + 1)
                v_.tensor_tensor(coef(p)[:, 0, 1, :], TU[:, 0:8], TB[:], ALU.subtract).then_inc(sem["cf1"], 1)

            def h_second1(dve, n, p):
                dve.wait_ge(sem["hm2"], n + 1)
                v_.tensor_tensor(A1[:], HM2[:, 0:512], HM2[:, 512:1024], ALU.add).then_inc(sem["a1"], 1)

            def h_second2(dve, n, p):
                dve.wait_ge(sem["a1"], n + 1)
                want(dve, "htp", n)
                v_.tensor_tensor(H12[:, RW:2 * RW], A1[:, 0:RW], A1[:, RW:2 * RW], ALU.add).then_inc(sem["h2"], 1)

            hz = HZ[:].rearrange("p (t k c) -> p t k c", t=2, k=2)

            def stream(dve, n, p):
                dve.wait_ge(sem["ow"], n + 1)
                dve.wait_ge(sem["res"], n + 1)
                want(dve, "ztp", n)
                v_.tensor_tensor(hz[:, :, 1, :], v3(XB[:, 0:128], C), v3(RES[p][:], C), ALU.add).then_inc(sem["yy"], 1)

            def stats2(dve, n, p):
                dve.wait_ge(sem["yy"], n + 1)
                for t in range(2):
                    last = v_.bn_stats(ST2[:, 6 * t:6 * t + 6], hz[:, t, 1, :])
                last.then_inc(sem["bs2"], 1)

            def mean_var2(dve, n, p):
                dve.wait_ge(sem["pbe"], 1)
                dve.wait_ge(sem["bs2"], n + 1)
                for t in range(2):
                    last = v_.bn_aggr(MV2[:, 2 * t:2 * t + 2], ST2[:, 6 * t:6 * t + 6])
                last.then_inc(sem["bv2"], 1)

            def radicand2(dve, n, p):
                dve.wait_ge(sem["bv2"], n + 1)
                want(dve, "rs2", n)
                v_.tensor_scalar(PW2[:], v3(MV2[:], 2)[:, :, 1], EPS, None, ALU.add).then_inc(sem["pw2"], 1)

            def shift2(dve, n, p):
                dve.wait_ge(sem["rs2"], n + 1)
                want(dve, "zz", n)
                v_.scalar_tensor_tensor(NB2[:], v3(MV2[:], 2)[:, :, 0], -1.0, RS2[:], ALU.mult,
                                        ALU.mult).then_inc(sem["nb2"], 1)

            def step(s, sp, half, live):
                if live(2):
                    elu(dve, s - 2, sp, 1)
                if live(1):
                    denominators(dve, s - 1, 1 - sp)
                if live(2):
                    qk_sums(dve, s - 2, sp)
                if live(3):
                    h_max(dve, s - 3, 1 - sp)
                if live(4):
                    stream(dve, s - 4, sp)
                if live(1):
                    ctx_norm(dve, s - 1, 1 - sp)
                if live(3):
                    h_query(dve, s - 3, 1 - sp)
                if live(4):
                    stats2(dve, s - 4, sp)
                if live(0):
                    rowmax(dve, s, sp, 0)
                if live(1):
                    hidden0(dve, s - 1, 1 - sp)
                    stats1(dve, s - 1, 1 - sp)
                if live(4):
                    mean_var2(dve, s - 4, sp)
                if live(1):
                    mean_var1(dve, s - 1, 1 - sp)
                if live(3):
                    coefs5(dve, s - 3, 1 - sp)
                if live(1):
                    radicand1(dve, s - 1, 1 - sp)
                if live(3):
                    query_dots(dve, s - 3, 1 - sp)
                if live(4):
                    radicand2(dve, s - 4, sp)
                if live(3):
                    query1(dve, s - 3, 1 - sp)
                if live(1):
                    shift1(dve, s - 1, 1 - sp)
                if live(3):
                    query2(dve, s - 3, 1 - sp)
                if live(0):
                    rowmax(dve, s, sp, 1)
                if live(3):
                    query3(dve, s - 3, 1 - sp)
                if live(2):
                    strengths(dve, s - 2, sp)
                if live(4):
                    shift2(dve, s - 4, sp)
                if live(3):
                    query4(dve, s - 3, 1 - sp)
                if live(2):
                    dots(dve, s - 2, sp)
                    inverses(dve, s - 2, sp)
                if live(1):
                    rk_max(dve, s - 1, 1 - sp)
                if live(2):
                    coefs1(dve, s - 2, sp)
                if live(1):
                    rk_sub(dve, s - 1, 1 - sp)
                if live(2):
                    coefs2(dve, s - 2, sp)
                if live(3):
                    h_second1(dve, s - 3, 1 - sp)
                if live(2):
                    coefs3(dve, s - 2, sp)
                if live(3):
                    h_second2(dve, s - 3, 1 - sp)
                if live(2):
                    coefs4(dve, s - 2, sp)
                if live(1):
                    rk_sums(dve, s - 1, 1 - sp)
                    elu(dve, s - 1, 1 - sp, 0)
            steps(step, dve)

            def select(dve, g, p):
                want(dve, "fme0", g - 1)
                for b in range(BLK):
                    e = dve.value_load(ROUTE[0:1, bass.ds(g * BLK + b, 1)], min_val=0, max_val=NE - 1)
                    last = v_.tensor_tensor(WSEL[p][:, 0, b, :], EXP[:, bass.ds(e * EW, EW)], SHR[:, 0:EW], ALU.add)
                last.then_inc(sem["fsel0"], 1)

            def finish(dve, g, p, pair):
                dve.wait_ge(sem["fo"], g + 1)
                want(dve, f"fst{p}", pair * 16)
                y = HZT[64:128, bass.ds(g * 512, 512)].rearrange("p (w n) -> p w n", w=8)
                for b in range(BLK):
                    last = v_.scalar_tensor_tensor(
                        v3(FO[p][:, b * 128:(b + 1) * 128], 16), v3(PO[p][64:128, b * 128:(b + 1) * 128], 16),
                        BO[64:128, 0:1], y[:, :, b * 16:(b + 1) * 16], ALU.add, ALU.add)
                last.then_inc(sem["foe"], 1)

            def feed(s, sp, half, live):
                if live(3):
                    finish(dve, s - 3, 1 - sp, half + sp - 2)
                if live(0):
                    select(dve, s, sp)
            dve.wait_ge(sem["hz"], TILES)
            steps(feed, dve, GROUPS, 3, 6)

        @block.tensor
        def _(pe):
            mm = nc.tensor.matmul
            tr = nc.tensor.transpose
            pe.wait_ge(sem["ldw"], 48)
            r5 = ROT[:].rearrange("p (v q t d) -> p v q t d", v=16, q=2, t=2)
            for t in range(2):
                for half in range(2):
                    last = mm(G[half][64 * t:64 * t + 64, :], WQK[:], r5[:, half * 8:(half + 1) * 8, :, t, :],
                              start=True, stop=True)
                last.then_inc(sem["wr"], 1)
            for v in range(16):
                last = mm(XA[:, v:v + 1], ROT[:, v * 128:(v + 1) * 128], BQK[:, 0:1], start=True, stop=True)
            last.then_inc(sem["qbm"], 1)
            pe.wait_ge(sem["wre"], 2)
            pe.wait_ge(sem["ldx"], 16)
            x5 = X2[:].rearrange("p (w r c) -> p w r c", r=8, c=8)
            for v in range(16):
                half, pos = v // 8, v % 8
                want(pe, f"qke{v % 2}", 2 * (v // 2))
                rhs = x5[:, :, pos, :] if half == 0 else x5[:, :, :, pos]
                mm(G[v % 2][:], WROT[:, v * 128:(v + 1) * 128], rhs, start=True, stop=True)\
                    .then_inc(sem[f"qkp{v % 2}"], 1)
            pe.wait_ge(sem["lds"], 16 * 13)
            for i, (b_, lo, hi) in enumerate(((S[0], 0, 512), (S[1], 512, 1024), (TP, 1024, WCOLS))):
                mm(b_[C:C + 1, 0:hi - lo], LNB[:, 0:1], WS[0:C, lo:hi], start=True, stop=True).then_inc(sem["wsb"], 1)
            pe.wait_ge(sem["bvb"], 1)
            pe.wait_ge(sem["zero"], 1)
            mm(XB[:, 0:C], BVB[:], PJ[0:C, 0:C], start=True, stop=False)
            mm(XB[:, 0:C], ONES[:], PROWB[:], start=False, stop=True).then_inc(sem["pbm"], 1)
            pe.wait_ge(sem["zro1"], 4)
            pe.wait_ge(sem["wss"], 1)
            pe.wait_ge(sem["ldp"], 48)

            def values(pe, n, p, pair):
                pe.wait_ge(sem[f"xt{p}"], pair * 16 + 16)
                want(pe, "ot", n)
                for w in range(2):
                    for e in range(2):
                        last = mm(XA[64 * e:64 * e + 64, w * 64:(w + 1) * 64], XT[p][:, w * 64:(w + 1) * 64],
                                  WV[:, e * 64:(e + 1) * 64], start=True, stop=True)
                last.then_inc(sem["vp"], 1)

            def scores(pe, n, p, w):
                pe.wait_ge(sem["qw"], n + 1)
                pe.wait_ge(sem[f"kb{w}"], n + 1)
                want(pe, f"ex{w}", n)
                mm(S[w][:], QW[p][:, w * 128:(w + 1) * 128], KB[p][w][:], start=True, stop=True)\
                    .then_inc(sem[f"sc{w}"], 1)

            def probsT(pe, n, p, w):
                pe.wait_ge(sem[f"ex{w}"], n + 1)
                want(pe, f"pt{1 - w}", n + w)
                for j in range(4):
                    last = tr(TP[:, j * 128:(j + 1) * 128], SX[w][:, j * 128:(j + 1) * 128], IDN[:])
                last.then_inc(sem[f"tp{w}"], 1)

            vb = VB[:].rearrange("p (w t j c) -> p w t j c", w=2, t=2, j=4)
            cx = CX[:, 0:144].rearrange("p (t j c) -> p t j c", t=2, j=4)

            def attend(pe, n, p, w):
                pe.wait_ge(sem[f"pt{w}"], n + 1)
                if w == 0:
                    pe.wait_ge(sem["vb"], n + 1)
                    want(pe, "cx", n)
                for t in range(2):
                    for j in range(4):
                        last = mm(cx[64 * w:64 * w + 64, t, j, :], PT[w][:, j * 128 + t * 64:j * 128 + t * 64 + 64],
                                  vb[:, w, t, j, :], start=True, stop=True)
                last.then_inc(sem[f"pv{w}"], 1)

            def ctxT(pe, n, p):
                pe.wait_ge(sem["cx"], n + 1)
                tr(XA[:, 128:256], CT[:], IDN[:]).then_inc(sem["ctp"], 1)

            def project(pe, n, p):
                pe.wait_ge(sem["ctt"], n + 1)
                mm(XA[:, 256:384], CTT[:], PJ[:], start=True, stop=True).then_inc(sem["pj"], 1)

            def obsT(pe, n, p):
                pe.wait_ge(sem["ldp"], 48)
                pe.wait_ge(sem["oh"], n + 1)
                for t in range(2):
                    last = tr(XA[0:C, t * 128:(t + 1) * 128], OH[:, t * C:(t + 1) * C], IDN[:])
                last.then_inc(sem["otp"], 1)

            def slow(pe, n, p, what, t):
                lo, wide = {"rk": (CRK, RW + 2 * RH), "qk": (CQK, 512), "v": (CV, 512)}[what]
                if what == "rk":
                    pe.wait_ge(sem["ot"], n + 1)
                    want(pe, f"vv{t}", n)
                elif what == "qk":
                    pe.wait_ge(sem[f"rsub{t}"], n + 1)
                else:
                    pe.wait_ge(sem[f"el{t}"], n + 1)
                mm(G[t][:, 0:wide], OT[p][:, t * 128:(t + 1) * 128], WS[:, lo:lo + wide], start=True, stop=True)\
                    .then_inc(sem[f"g{what}{t}"], 1)

            def hT(pe, n, p):
                pe.wait_ge(sem["h2"], n + 1)
                pe.wait_ge(sem["h1"], n + 1)
                want(pe, "hz", n)
                for c in range(2):
                    for t in range(2):
                        k = (c * 2 + t) * 128
                        last = tr(XB[:, k:k + 128], H12[:, t * RW + c * 128:t * RW + c * 128 + 128], IDN[:])
                last.then_inc(sem["htp"], 1)

            def output(pe, n, p):
                pe.wait_ge(sem["ht"], n + 1)
                for t in range(2):
                    for c in range(2):
                        k = (c * 2 + t) * 128
                        last = mm(XB[:, t * C:(t + 1) * C], HT[:, k:k + 128], OW[:, c * C:(c + 1) * C],
                                  start=(c == 0), stop=(c == 1))
                last.then_inc(sem["ow"], 1)

            def hzT(pe, n, p):
                pe.wait_ge(sem["zz"], n + 1)
                for t in range(2):
                    last = tr(XB[:, 256 + t * 128:384 + t * 128], HZ[:, t * 128:(t + 1) * 128], IDN[:])
                last.then_inc(sem["ztp"], 1)

            def step(s, sp, half, live):
                if live(0):
                    scores(pe, s, sp, 0)
                if live(1):
                    ctxT(pe, s - 1, 1 - sp)
                    project(pe, s - 1, 1 - sp)
                if live(2):
                    slow(pe, s - 2, sp, "v", 0)
                    slow(pe, s - 2, sp, "v", 1)
                if live(0):
                    scores(pe, s, sp, 1)
                    probsT(pe, s, sp, 0)
                if live(1):
                    obsT(pe, s - 1, 1 - sp)
                    slow(pe, s - 1, 1 - sp, "rk", 1)
                    slow(pe, s - 1, 1 - sp, "rk", 0)
                if live(0):
                    values(pe, s, sp, half)
                    probsT(pe, s, sp, 1)
                    attend(pe, s, sp, 0)
                if live(4):
                    hzT(pe, s - 4, sp)
                if live(1):
                    slow(pe, s - 1, 1 - sp, "qk", 0)
                    slow(pe, s - 1, 1 - sp, "qk", 1)
                if live(3):
                    hT(pe, s - 3, 1 - sp)
                if live(0):
                    attend(pe, s, sp, 1)
                if live(3):
                    output(pe, s - 3, 1 - sp)
            steps(step, pe)

            def hidden(pe, g, p):
                want(pe, "fhe", g - 1)
                mm(PH[p][:], WI[:], HZT[0:C, bass.ds(g * 512, 512)], start=True, stop=True).then_inc(sem["fh"], 1)

            def expert0(pe, g, p):
                pe.wait_ge(sem["fhe"], g + 1)
                pe.wait_ge(sem["fsel0"], g + 1)
                want(pe, "fme0", g - 1)
                fa = FA[p].rearrange("p (w n) -> p w n", w=8)
                for b in range(BLK):
                    last = mm(v3(P0[p][:, b * 128:(b + 1) * 128], 16), WSEL[p][:, 0, b, 0:HID],
                              fa[:, :, b * 16:(b + 1) * 16], start=True, stop=True)
                last.then_inc(sem["fm0"], 1)

            def expert1(pe, g, p):
                pe.wait_ge(sem["fme0"], g + 1)
                pe.wait_ge(sem["fsel1"], g + 1)
                want(pe, "fme1", g - 1)
                for b in range(BLK):
                    last = mm(P1[p][:, b * 128:(b + 1) * 128], WSEL[p][:, 1, b, 0:HID],
                              FB[p][:, b * 128:(b + 1) * 128], start=True, stop=True)
                last.then_inc(sem["fm1"], 1)

            def result(pe, g, p):
                pe.wait_ge(sem["fme1"], g + 1)
                want(pe, "foe", g - 1)
                mm(PO[p][64:128, :], WO[:], FC[p], start=True, stop=True).then_inc(sem["fo"], 1)

            def feed(s, sp, half, live):
                if live(0):
                    hidden(pe, s, sp)
                if live(1):
                    expert0(pe, s - 1, 1 - sp)
                if live(2):
                    expert1(pe, s - 2, sp)
                if live(3):
                    result(pe, s - 3, 1 - sp)
            pe.wait_ge(sem["hz"], TILES)
            pe.wait_ge(sem["lde"], 112)
            steps(feed, pe, GROUPS, 3, 6)


def _rotations():
    rot = np.zeros((128, 16, 2, 2, NH * 4), np.float32)
    half = HD // 2
    inv = 1.0 / 10000.0 ** (np.arange(0, half, 2, dtype=np.float32) / half)
    for v in range(16):
        for qk in range(2):
            scale = HD ** -0.5 if qk == 0 else 1.0
            for h in range(NH):
                for f in range(2):
                    a = np.float32(v % 8) * inv[f]
                    c, s = scale * np.cos(a), scale * np.sin(a)
                    src = qk * 64 + h * HD + (v // 8) * half + 2 * f
                    dst = h * 4 + 2 * f
                    rot[src, v, qk, :, dst] = c
                    rot[src + 1, v, qk, :, dst] = -s
                    rot[src, v, qk, :, dst + 1] = s
                    rot[src + 1, v, qk, :, dst + 1] = c
    return rot.reshape(128, 16 * 128)


def kernel(x, L0_tok_qkv_w, L0_tok_qkv_b, L0_tok_proj_w, L0_tok_proj_b, L0_attn_slow_W, L0_attn_out_W,
           L0_attn_ln_g, L0_attn_ln_b, L0_ffn_route_id, L0_ffn_Wi, L0_ffn_bi, L0_ffn_Wr, L0_ffn_br,
           L0_ffn_Ws, L0_ffn_bs, L0_ffn_Wo, L0_ffn_bo):
    import concourse.bacc as bacc
    from concourse.bass_utils import run_bass_kernel_spmd

    x, qkv_w, qkv_b, proj_w, proj_b, slow, outw, ln_g, ln_b, route, Wi, bi, Wr, br, Ws, bs, Wo, bo = (
        np.asarray(a) for a in (x, L0_tok_qkv_w, L0_tok_qkv_b, L0_tok_proj_w, L0_tok_proj_b, L0_attn_slow_W,
                                L0_attn_out_W, L0_attn_ln_g, L0_attn_ln_b, L0_ffn_route_id, L0_ffn_Wi,
                                L0_ffn_bi, L0_ffn_Wr, L0_ffn_br, L0_ffn_Ws, L0_ffn_bs, L0_ffn_Wo, L0_ffn_bo))
    x2 = x.reshape(B, 8, 8, 8, 8, C).transpose(0, 5, 1, 3, 2, 4).reshape(B * C, TOK)
    wv = qkv_w[128:192].reshape(4, 2, HD, C).transpose(3, 1, 0, 2).reshape(C, C)
    sw = slow.reshape(RH, 5 * RD + 2, C)
    fields = [sw[:, i * RD:(i + 1) * RD].reshape(RW, C) for i in range(5)]
    slowT = np.concatenate([fields[0], fields[1], fields[2], fields[4], fields[3], sw[:, 5 * RD], sw[:, 5 * RD + 1]]).T
    experts = np.concatenate([Wr.transpose(3, 0, 1, 2), br.transpose(2, 0, 1)[..., None]], -1).reshape(HID, -1)
    shared = np.concatenate([Ws[:, 0].transpose(2, 0, 1), bs[:, 0].T[..., None]], -1).reshape(HID, -1)
    p = np.arange(128)
    ins = dict(
        x2=x2, wqk=qkv_w[0:128], wv=wv, bqk=qkv_b[0:128, None], bv=qkv_b[128:192, None], projT=proj_w.T,
        projb=proj_b[None], rot=_rotations(),
        mask_img=((p[:, None] // 32) % 2 == np.arange(2)).astype(np.float32),
        mask_head=((p[:, None] % 32) // 4 == np.arange(NH)).astype(np.float32),
        ident_in=np.eye(128, dtype=np.float32), slowT=slowT, outT=outw.T, ln_g=ln_g[:, None], ln_b=ln_b[:, None],
        route=route[None], wiT=Wi.T, bi=bi[:, None], experts=experts, shared=shared, woT=Wo.T, bo=bo[:, None])
    nc = bacc.Bacc("TRN2", target_bir_lowering=False, num_devices=1)
    arrays, args = {}, []
    for name, a in ins.items():
        a = np.ascontiguousarray(a)
        arrays[f"in_{name}"] = a
        args.append(nc.dram_tensor(f"in_{name}", a.shape, mybir.dt.from_np(a.dtype), kind="ExternalInput").ap())
    out = nc.dram_tensor("out_0", (GROUPS, C, 512), F32, kind="ExternalOutput").ap()
    vit_tower(nc, *args, out)
    r = run_bass_kernel_spmd(nc, [arrays], core_ids=[0])
    y = r.results[0]["out_0"]
    y = y.reshape(B, 8, C, BLK, 8, 2, 8).transpose(0, 1, 3, 5, 4, 6, 2)
    return np.ascontiguousarray(y.reshape(B, TOK, C))
```

```python
from contextlib import ExitStack

import concourse.bass as bass
import numpy as np
from concourse import mybir

F32 = mybir.dt.float32
ALU = mybir.AluOpType
ACT = mybir.ActivationFunctionType
AX = mybir.AxisListType

B, HH, WW, C = 2, 64, 64, 64
WIN = 8
NTOK = WIN * WIN
NWIN = (HH // WIN) * (WW // WIN)
TILES = NWIN // 2
NH, HD = 8, 8
RH, RD = 8, 32
RW = RH * RD
HID, NE, NL = 128, 16, 2
EPS = 1e-5
TOK = HH * WW
GROUPS = 16
BLK = 4
EW = HID + 1
CQK, CV, CRK = 0, 2 * RW, 4 * RW
WCOLS = 5 * RW + 2 * RH
LAG = 6
LOOP_FROM = 8


def vit_tower(nc, x2, wqk, wv, bqk, bv, projT, projb, rot, mask_img, mask_head, ident_in,
              slowT, outT, ln_g, ln_b, route, wiT, bi, experts, shared, woT, bo, out):
    ctx = ExitStack()
    with ctx:
        def sb(name, shape):
            return ctx.enter_context(nc.sbuf_tensor(name, shape, F32))

        def bank(name):
            return ctx.enter_context(nc.psum_tensor(name, [128, 512], F32))

        IDN = sb("IDN", [128, 128])
        MIMG = sb("MIMG", [128, 2])
        MHEAD = sb("MHEAD", [128, NH])
        ROT = sb("ROT", [128, 16 * 64])
        WQK = sb("WQK", [128, C])
        BQK = sb("BQK", [128, 1])
        WROT = sb("WROT", [128, 16 * 128])
        QB = sb("QB", [128, 16])
        WV = sb("WV", [128, 2 * 64])
        PJ = sb("PJ", [128, 128])
        BV = sb("BV", [C, 1])
        BVB = sb("BVB", [C, 128])
        PROWB = sb("PROWB", [1, C])
        ONES = sb("ONES", [1, 128])
        PBIAS = sb("PBIAS", [128, 2 * C])
        WS = sb("WS", [C + 1, WCOLS])
        LNG = sb("LNG", [C, 1])
        LNB = sb("LNB", [C, 1])
        OW = sb("OW", [128, 2 * C])
        HALF = sb("HALF", [128, 4])
        NEG1 = sb("NEG1", [128, 1])
        ROUTE = ctx.enter_context(nc.sbuf_tensor("ROUTE", [1, 64], mybir.dt.int32))
        WI = sb("WI", [C, HID])
        BI = sb("BI", [HID, 1])
        EXP = sb("EXP", [128, NL * NE * EW])
        SHR = sb("SHR", [128, NL * EW])
        WO = sb("WO", [HID, C])
        BO = sb("BO", [128, 1])
        X2 = sb("X2", [128, TOK])
        Q2 = sb("Q2", [128, TOK])
        K2 = sb("K2", [128, TOK])
        HZT = sb("HZT", [128, B * TOK])
        XT = [sb(f"XT{p}", [128, 128]) for p in range(2)]
        QW = [sb(f"QW{p}", [128, 2 * 128]) for p in range(2)]
        KB = [[sb(f"KB{p}{w}", [128, 512]) for w in range(2)] for p in range(2)]
        NMX = [sb(f"NMX{w}", [128, NH]) for w in range(2)]
        SX = [sb(f"SX{w}", [128, 512]) for w in range(2)]
        PT = [sb(f"PT{w}", [128, 512]) for w in range(2)]
        VB = sb("VB", [128, 2 * 8 * 18])
        RDEN = sb("RDEN", [128, 16])
        CT = sb("CT", [128, 128])
        CTT = sb("CTT", [128, 128])
        ST1 = sb("ST1", [128, 12])
        MV1 = sb("MV1", [128, 4])
        PW1 = sb("PW1", [128, 4])
        RS1 = sb("RS1", [128, 4])
        NB1 = sb("NB1", [128, 4])
        RA = sb("RA", [128, 2])
        OH = sb("OH", [128, 128])
        RES = [sb(f"RES{p}", [128, 128]) for p in range(2)]
        OT = [sb(f"OT{p}", [C + 1, 256]) for p in range(2)]
        MR = sb("MR", [128, 2 * RH])
        TH = sb("TH", [128, 32])
        BE = sb("BE", [128, 32])
        EQ = [sb(f"EQ{t}", [128, 512]) for t in range(2)]
        QK = sb("QK", [128, 2 * 512])
        RK = [sb(f"RK{p}", [128, 2 * RW]) for p in range(2)]
        V = [sb(f"V{p}", [128, 2 * 512]) for p in range(2)]
        PR = sb("PR", [128, 5 * RW])
        SM = sb("SM", [128, 48])
        RC = sb("RC", [128, 48])
        DT = sb("DT", [128, 40])
        NM = sb("NM", [128, 40])
        CC = [sb(f"CC{p}", [128, 16]) for p in range(2)]
        CF = [sb(f"CF{p}", [128, 32]) for p in range(2)]
        UU = [sb(f"UU{p}", [128, 16]) for p in range(2)]
        GG = [sb(f"GG{p}", [128, 8]) for p in range(2)]
        TA = sb("TA", [128, 8])
        BK = sb("BK", [128, 16])
        HM = sb("HM", [128, 512])
        H1 = sb("H1", [128, RW])
        MH = sb("MH", [128, RH])
        QX = sb("QX", [128, RW])
        PQ = sb("PQ", [128, 3 * RW])
        DQ = sb("DQ", [128, 24])
        RQ = sb("RQ", [128, 8])
        TU = sb("TU", [128, 16])
        TB = sb("TB", [128, 8])
        HM2 = sb("HM2", [128, 1024])
        HT = sb("HT", [128, 512])
        HZ = sb("HZ", [128, 256])
        ST2 = sb("ST2", [128, 12])
        MV2 = sb("MV2", [128, 4])
        PW2 = sb("PW2", [128, 2])
        RS2 = sb("RS2", [128, 2])
        NB2 = sb("NB2", [128, 2])
        space = [X2[:, 0:8 * EW], X2[:, 8 * EW:16 * EW], X2[:, 16 * EW:24 * EW], K2[:, 1024:1024 + 8 * EW]]
        WSEL = [a.rearrange("p (b e) -> p b e", b=BLK) for a in space]
        FA = [Q2[:, p * 512:(p + 1) * 512] for p in range(2)]
        FB = [Q2[:, 1024 + p * 512:1536 + p * 512] for p in range(2)]
        FC = [Q2[:, 2048 + p * 512:2560 + p * 512] for p in range(2)]
        FO = [K2[64:128, p * 512:(p + 1) * 512] for p in range(2)]

        S = [bank("S0"), bank("S1")]
        TP = bank("TP")
        CX = bank("CX")
        XA = bank("XA")
        XB = bank("XB")
        G = [bank("G0"), bank("G1")]
        PQK = [G[0], G[1], S[0], S[1]]
        PH, P0, P1, PO = S, G, [TP, CX], [XA, XB]

        names = """ldw ldx ldp lds lde zero zro1 wr wre qbm qbe qkp0 qkp1 qke0 qke1 bvb pbm pbe wsb wss shi setd xt0
            xt1 qw kb0 kb1 vp vb sc0 sc1 mx0 mx1 ex0 ex1 tp0 tp1 pt0 pt1 pv0 pv1 rd cx ctp ctt pj bs1 bv1 pw1
            rs1 nb1 oh res otp ot grk0 grk1 gqk0 gqk1 gv0 gv1 mr rsub0 rsub1 rk0 rk1 th eq0 eq1 el0 el1 vv0
            vv1 pra prr sq sr rp rc be n1 n2 n3 cc cf0 hm h1 mh qx qr pq dq rq t1 t2 cf1 hm2 htp ht ow yy bs2
            bv2 pw2 rs2 nb2 zz ztp hz fsel0 fsel1 fh fhe fm0 fme0 fm1 fme1 fo foe fst0 fst1""".split()
        sem = {n: ctx.enter_context(nc.semaphore("s_" + n)) for n in names}

        def want(eng, name, n):
            if not isinstance(n, int) or n > 0:
                eng.wait_ge(sem[name], n)

        def v3(ap, b):
            return ap.rearrange("p (a b) -> p a b", b=b)

        def over(ap, k):
            return ap.unsqueeze(2).to_broadcast([ap.shape[0], ap.shape[1], k])

        def steps(step, eng, count=TILES, lag=LAG, loop_from=LOOP_FROM, unroll=2):
            for s in range(loop_from):
                step(s, s % unroll, s // unroll, lambda k, s=s: 0 <= s - k < count)
            with eng.Fori(loop_from // unroll, count // unroll) as i:
                for p in range(unroll):
                    step(i * unroll + p, p, i, lambda k: True)
            for s in range(count, count + lag):
                step(s, s % unroll, s // unroll, lambda k, s=s: 0 <= s - k < count)

        wrot = WROT[:].rearrange("p (v q t d) -> p v q t d", v=16, q=2, t=2)

        def diagonal(eng, copy, half):
            for t in range(2):
                eng.wait_ge(sem["wr"], 2 * t + half + 1)
                for qk in range(2):
                    last = copy(wrot[64 * t:64 * t + 64, half * 8:(half + 1) * 8, qk, t, :],
                                G[half][64 * t:64 * t + 64, :].rearrange("p (v q d) -> p v q d", v=8, q=2)[:, :, qk, :])
                last.then_inc(sem["wre"], 1)
        block = ctx.enter_context(nc.Block())

        @block.sync
        def _(sp):
            sp.dma_start(WQK[:], wqk).then_inc(sem["ldw"], 16)
            sp.dma_start(BQK[:], bqk).then_inc(sem["ldw"], 16)
            sp.dma_start(ROT[:], rot).then_inc(sem["ldw"], 16)
            sp.dma_start(X2[:], x2).then_inc(sem["ldx"], 16)
            sp.dma_start(MIMG[:], mask_img).then_inc(sem["ldp"], 16)
            sp.dma_start(MHEAD[:], mask_head).then_inc(sem["ldp"], 16)
            sp.dma_start(IDN[:], ident_in).then_inc(sem["ldp"], 16)
            sp.wait_ge(sem["zero"], 1)
            for t in range(2):
                for e in range(2):
                    sp.dma_start(WV[64 * t:64 * t + 64, e * 64 + t * 32:e * 64 + t * 32 + 32],
                                 wv[:, e * 32:(e + 1) * 32]).then_inc(sem["lds"], 16)
                sp.dma_start(PJ[64 * t:64 * t + 64, t * C:(t + 1) * C], projT).then_inc(sem["lds"], 16)
            sp.dma_start(BV[:], bv).then_inc(sem["lds"], 16)
            sp.dma_start(PROWB[:], projb).then_inc(sem["lds"], 16)
            sp.dma_start(WS[0:C, :], slowT).then_inc(sem["lds"], 16)
            sp.dma_start(LNG[:], ln_g).then_inc(sem["lds"], 16)
            sp.dma_start(LNB[:], ln_b).then_inc(sem["lds"], 16)
            for c in range(2):
                sp.dma_start(OW[:, c * C:(c + 1) * C], outT[c * 128:(c + 1) * 128, :]).then_inc(sem["lds"], 16)
            sp.dma_start(WI[:], wiT).then_inc(sem["lde"], 16)
            sp.dma_start(BI[:], bi).then_inc(sem["lde"], 16)
            sp.dma_start(WO[:], woT).then_inc(sem["lde"], 16)
            sp.dma_start(BO[64:128, :], bo).then_inc(sem["lde"], 16)
            sp.dma_start(ROUTE[:], route).then_inc(sem["lde"], 16)
            sp.dma_start(SHR[:], shared).then_inc(sem["lde"], 16)
            sp.dma_start(EXP[:], experts).then_inc(sem["lde"], 16)

            def load_tile(sp, n, p):
                want(sp, "vp", n - 1)
                sp.dma_start(XT[p][:], x2[:, bass.ds(n * 128, 128)]).then_inc(sem[f"xt{p}"], 16)
            load_tile(sp, 0, 0)
            load_tile(sp, 1, 1)
            with sp.Fori(1, TILES // 2) as i:
                load_tile(sp, i * 2, 0)
                load_tile(sp, i * 2 + 1, 1)
            sp.wait_ge(sem["foe"], 1)
            sp.dma_start(out[0], FO[0]).then_inc(sem["fst0"], 16)
            sp.wait_ge(sem["foe"], 2)
            sp.dma_start(out[1], FO[1]).then_inc(sem["fst1"], 16)
            with sp.Fori(1, GROUPS // 2) as g:
                for p in range(2):
                    sp.wait_ge(sem["foe"], g * 2 + (p + 1))
                    sp.dma_start(out[bass.ds(g * 2 + p, 1)].rearrange("a c n -> (a c) n"), FO[p])\
                        .then_inc(sem[f"fst{p}"], 16)
            sp.wait_ge(sem["fst0"], 8 * GROUPS)
            sp.wait_ge(sem["fst1"], 8 * GROUPS)

        @block.gpsimd
        def _(pool):
            pool.wait_ge(sem["ldp"], 48)
            pool.wait_ge(sem["zro1"], 3)

            def prepare(pool, n, p):
                want(pool, "sc1", n - 1)
                nc.gpsimd.tensor_tensor(
                    QW[p][:].rearrange("p (w t q) -> p w t q", w=2, t=2),
                    Q2[:, bass.ds(n * 128, 128)].rearrange("p (w q) -> p w q", w=2).unsqueeze(2)
                    .to_broadcast([128, 2, 2, NTOK]),
                    MIMG[:].unsqueeze(1).unsqueeze(3).to_broadcast([128, 2, 2, NTOK]),
                    ALU.mult).then_inc(sem["qw"], 1)
                for w in range(2):
                    nc.gpsimd.tensor_tensor(
                        v3(KB[p][w][:], NTOK),
                        K2[:, bass.ds(n * 128 + w * 64, 64)].unsqueeze(1).to_broadcast([128, NH, NTOK]),
                        over(MHEAD[:], NTOK), ALU.mult).then_inc(sem[f"kb{w}"], 1)

            def rsqrt1(pool, n, p):
                pool.wait_ge(sem["pw1"], n + 1)
                want(pool, "oh", n)
                want(pool, "nb1", n)
                nc.gpsimd.tensor_tensor(RS1[:], PW1[:], HALF[:], ALU.pow).then_inc(sem["rs1"], 1)

            def products(pool, n, p):
                qk = QK[:]
                want(pool, "rp", n)
                pool.wait_ge(sem["el0"], n + 1)
                nc.gpsimd.tensor_tensor(PR[:, 2 * RW:3 * RW], qk[:, 0:RW], qk[:, RW:2 * RW], ALU.mult)
                pool.wait_ge(sem["el1"], n + 1)
                nc.gpsimd.tensor_tensor(v3(PR[:, 0:2 * RW], RW), v3(qk[:, 2 * RW:4 * RW], RW),
                                        qk[:, RW:2 * RW].unsqueeze(1).to_broadcast([128, 2, RW]), ALU.mult)
                nc.gpsimd.tensor_tensor(PR[:, 3 * RW:4 * RW], qk[:, 2 * RW:3 * RW], qk[:, 3 * RW:4 * RW],
                                        ALU.mult).then_inc(sem["pra"], 1)

            def key_product(pool, n, p):
                pool.wait_ge(sem["rk0"], n + 1)
                pool.wait_ge(sem["rk1"], n + 1)
                want(pool, "rp", n)
                nc.gpsimd.tensor_tensor(PR[:, 4 * RW:5 * RW], RK[p][:, 0:RW], RK[p][:, RW:2 * RW],
                                        ALU.mult).then_inc(sem["prr"], 1)

            def first_state(pool, n, p):
                pool.wait_ge(sem["cc"], n + 1)
                pool.wait_ge(sem["vv0"], n + 1)
                want(pool, "h1", n)
                nc.gpsimd.tensor_tensor(v3(HM[:], RD), v3(V[p][:, 0:512], RD), over(CC[p][:], RD),
                                        ALU.mult).then_inc(sem["hm"], 1)

            def state_sum(pool, n, p):
                pool.wait_ge(sem["hm"], n + 1)
                want(pool, "htp", n)
                nc.gpsimd.tensor_tensor(H1[:], HM[:, 0:RW], HM[:, RW:2 * RW], ALU.add).then_inc(sem["h1"], 1)

            def query_products(pool, n, p):
                pool.wait_ge(sem["qr"], n + 1)
                nc.gpsimd.tensor_tensor(v3(PQ[:, RW:3 * RW], RW), v3(RK[p][:], RW),
                                        PQ[:, 0:RW].unsqueeze(1).to_broadcast([128, 2, RW]),
                                        ALU.mult).then_inc(sem["pq"], 1)

            def second_state(pool, n, p):
                pool.wait_ge(sem["cf1"], n + 1)
                pool.wait_ge(sem["vv1"], n + 1)
                want(pool, "htp", n)
                nc.gpsimd.tensor_tensor(v3(HM2[:], RD), v3(V[p][:], RD), over(CF[p][:], RD),
                                        ALU.mult).then_inc(sem["hm2"], 1)

            def rsqrt2(pool, n, p):
                pool.wait_ge(sem["pw2"], n + 1)
                want(pool, "zz", n)
                nc.gpsimd.tensor_tensor(RS2[:], PW2[:], HALF[:, 0:2], ALU.pow).then_inc(sem["rs2"], 1)

            pool.wait_ge(sem["qke0"], 16)
            pool.wait_ge(sem["qke1"], 16)
            def step(s, sp, half, live):
                if live(1):
                    prepare(pool, s - 1, 1 - sp)
                if live(5):
                    query_products(pool, s - 5, 1 - sp)
                if live(6):
                    rsqrt2(pool, s - 6, sp)
                if live(4):
                    products(pool, s - 4, sp)
                if live(3):
                    rsqrt1(pool, s - 3, 1 - sp)
                if live(4):
                    key_product(pool, s - 4, sp)
                if live(5):
                    second_state(pool, s - 5, 1 - sp)
                if live(4):
                    first_state(pool, s - 4, sp)
                    state_sum(pool, s - 4, sp)
            steps(step, pool)

            pool.wait_ge(sem["lde"], 112)
            pool.wait_ge(sem["shi"], 1)
            pool.wait_ge(sem["ztp"], TILES)

            def select(pool, g, q):
                want(pool, "fme1", g - 3)
                for b in range(BLK // 2):
                    e = pool.value_load(ROUTE[0:1, bass.ds(g * BLK + b, 1)], min_val=0, max_val=NE - 1)
                    last = nc.gpsimd.tensor_tensor(WSEL[q][:, b, :], EXP[:, bass.ds(e * (NL * EW), NL * EW)], SHR[:],
                                                   ALU.add)
                last.then_inc(sem["fsel0"], 1)

            def feed(s, sp, half, live):
                if live(0):
                    select(pool, s, sp)
            steps(feed, pool, GROUPS, 0, 8, 4)

        @block.scalar
        def _(act):
            a_ = nc.scalar.activation
            act.wait_ge(sem["zro1"], 3)
            a_(TH[:, 0:1], NEG1[:], ACT.Exp)
            diagonal(act, nc.scalar.copy, 0)
            act.wait_ge(sem["qbm"], 1)
            a_(QB[:], XA[:, 0:16], ACT.Copy).then_inc(sem["qbe"], 1)
            act.wait_ge(sem["qbe"], 1)
            for v in range(0, 16, 2):
                act.wait_ge(sem["qkp0"], v // 2 + 1)
                half, pos = v // 8, v % 8
                for qk, dst in ((0, Q2), (1, K2)):
                    d = dst[64 * half:64 * half + 64, :].rearrange("p (w r c) -> p w r c", r=8, c=8)
                    d = d[:, :, pos, :] if half == 0 else d[:, :, :, pos]
                    a_(d, v3(PQK[v % 4][64 * qk:64 * qk + 64, :], 8), ACT.Identity,
                       bias=QB[64 * qk:64 * qk + 64, v:v + 1]).then_inc(sem["qke0"], 1)
            act.wait_ge(sem["pbm"], 1)
            for t in range(2):
                last = a_(PBIAS[:, t * C:(t + 1) * C], XA[:, 0:C], ACT.Copy)
            last.then_inc(sem["pbe"], 1)
            act.wait_ge(sem["zro1"], 4)

            vb = VB[:].rearrange("p (a c) -> p a c", c=18)

            def values(act, n, p):
                act.wait_ge(sem["vp"], n + 1)
                want(act, "pv1", n)
                for e in range(2):
                    last = a_(vb[64 * e:64 * e + 64, :, 9 * e:9 * e + 8],
                              v3(XA[64 * e:64 * e + 64, 0:128], 8), ACT.Copy)
                last.then_inc(sem["vb"], 1)

            def exps(act, n, p, w):
                act.wait_ge(sem[f"mx{w}"], n + 1)
                want(act, f"tp{w}", n)
                for h in range(NH):
                    last = a_(SX[w][:, h * NTOK:(h + 1) * NTOK], S[w][:, h * NTOK:(h + 1) * NTOK], ACT.Exp,
                              bias=NMX[w][:, h:h + 1])
                last.then_inc(sem[f"ex{w}"], 1)

            def probsT(act, n, p, w):
                act.wait_ge(sem[f"tp{w}"], n + 1)
                want(act, f"pv{w}", n)
                a_(PT[w][:], TP[:], ACT.Copy).then_inc(sem[f"pt{w}"], 1)

            def ctxT(act, n, p):
                act.wait_ge(sem["ctp"], n + 1)
                want(act, "pj", n)
                a_(CTT[:], XA[:, 128:256], ACT.Copy).then_inc(sem["ctt"], 1)

            def normed1(act, n, p):
                act.wait_ge(sem["nb1"], n + 1)
                want(act, "otp", n)
                for t in range(2):
                    last = a_(OH[:, 64 * t:64 * t + 64], CX[:, 256 + 64 * t:320 + 64 * t], ACT.Identity,
                              scale=RS1[:, 2 * t:2 * t + 1], bias=NB1[:, 2 * t:2 * t + 1])
                last.then_inc(sem["oh"], 1)

            def residual(act, n, p):
                act.wait_ge(sem["nb1"], n + 1)
                want(act, "ow", n - 1)
                for t in range(2):
                    last = a_(RES[p][:, 64 * t:64 * t + 64], CX[:, 256 + 64 * t:320 + 64 * t], ACT.Identity,
                              scale=RA[:, t:t + 1], bias=NB1[:, 2 * t + 1:2 * t + 2])
                last.then_inc(sem["res"], 1)

            hz = HZ[:].rearrange("p (t k c) -> p t k c", t=2, k=2)

            def stream(act, n, p):
                act.wait_ge(sem["bs2"], n + 1)
                want(act, "ztp", n)
                a_(hz[:, :, 1, :], v3(XB[:, 0:128], C), ACT.Copy).then_inc(sem["yy"], 1)

            def normed2(act, n, p):
                act.wait_ge(sem["nb2"], n + 1)
                want(act, "ztp", n)
                for t in range(2):
                    last = a_(hz[:, t, 0, :], XB[:, 64 * t:64 * t + 64], ACT.Identity, scale=RS2[:, t:t + 1],
                              bias=NB2[:, t:t + 1])
                last.then_inc(sem["zz"], 1)

            def obsT(act, n, p):
                act.wait_ge(sem["otp"], n + 1)
                want(act, "gv1", n - 1)
                a_(OT[p][0:C, :], XA[0:C, 0:256], ACT.Copy).then_inc(sem["ot"], 1)

            def rk_exp(act, n, p, t):
                act.wait_ge(sem[f"rsub{t}"], n + 1)
                a_(RK[p][:, t * RW:(t + 1) * RW], RK[p][:, t * RW:(t + 1) * RW], ACT.Exp).then_inc(sem[f"rk{t}"], 1)

            def gates(act, n, p):
                want(act, "be", n)
                for t in range(2):
                    act.wait_ge(sem[f"rsub{t}"], n + 1)
                    last = a_(TH[:, t * 16:(t + 1) * 16], G[t][:, RW:RW + 16], ACT.Tanh, scale=0.5)
                last.then_inc(sem["th"], 1)

            def qk_exp(act, n, p, t):
                act.wait_ge(sem[f"gqk{t}"], n + 1)
                want(act, f"el{t}", n)
                a_(EQ[t][:], G[t][:], ACT.Exp, bias=NEG1[:, 0:1]).then_inc(sem[f"eq{t}"], 1)

            def v_copy(act, n, p, t):
                act.wait_ge(sem[f"gv{t}"], n + 1)
                want(act, "hm2", n - 1)
                a_(V[p][:, t * 512:(t + 1) * 512], G[t][:], ACT.Copy).then_inc(sem[f"vv{t}"], 1)

            def query_exp(act, n, p):
                act.wait_ge(sem["qx"], n + 1)
                want(act, "dq", n)
                want(act, "pq", n)
                a_(PQ[:, 0:RW], QX[:], ACT.Exp).then_inc(sem["qr"], 1)

            def hT(act, n, p):
                act.wait_ge(sem["htp"], n + 1)
                want(act, "ow", n)
                a_(HT[:], XB[:], ACT.Copy).then_inc(sem["ht"], 1)

            def hzT(act, n, p):
                act.wait_ge(sem["ztp"], n + 1)
                a_(HZT[:].rearrange("p (t c) -> p t c", t=2)[:, :, bass.ds(n * 128, 128)],
                   v3(XB[:, 256:512], 128), ACT.Copy).then_inc(sem["hz"], 1)

            act.wait_ge(sem["ldp"], 48)
            def step(s, sp, half, live):
                if live(4):
                    residual(act, s - 4, sp)
                if live(5):
                    query_exp(act, s - 5, 1 - sp)
                if live(4):
                    qk_exp(act, s - 4, sp, 0)
                if live(3):
                    ctxT(act, s - 3, 1 - sp)
                if live(2):
                    exps(act, s - 2, sp, 1)
                if live(6):
                    stream(act, s - 6, sp)
                if live(2):
                    probsT(act, s - 2, sp, 0)
                if live(4):
                    v_copy(act, s - 4, sp, 0)
                if live(6):
                    normed2(act, s - 6, sp)
                if live(3):
                    normed1(act, s - 3, 1 - sp)
                if live(4):
                    v_copy(act, s - 4, sp, 1)
                if live(3):
                    obsT(act, s - 3, 1 - sp)
                if live(6):
                    hzT(act, s - 6, sp)
                if live(1):
                    exps(act, s - 1, 1 - sp, 0)
                if live(2):
                    probsT(act, s - 2, sp, 1)
                if live(3):
                    gates(act, s - 3, 1 - sp)
                if live(5):
                    hT(act, s - 5, 1 - sp)
                if live(2):
                    values(act, s - 2, sp)
                if live(3):
                    rk_exp(act, s - 3, 1 - sp, 0)
                    rk_exp(act, s - 3, 1 - sp, 1)
                    qk_exp(act, s - 3, 1 - sp, 1)
            steps(step, act)

            def relu0(act, g, p):
                act.wait_ge(sem["fh"], g + 1)
                want(act, "fm0", g - 1)
                a_(FA[p], PH[p][:], ACT.Relu, bias=BI[:, 0:1]).then_inc(sem["fhe"], 1)

            def relu1(act, g, p, q):
                act.wait_ge(sem["fm0"], g + 1)
                want(act, "fm1", g - 1)
                for b in range(BLK):
                    last = a_(FB[p][:, b * 128:(b + 1) * 128], P0[p][:, b * 128:(b + 1) * 128], ACT.Relu,
                              bias=WSEL[q][:, b, HID:HID + 1])
                last.then_inc(sem["fme0"], 1)

            def relu2(act, g, p, q):
                act.wait_ge(sem["fm1"], g + 1)
                want(act, "fo", g - 1)
                for b in range(BLK):
                    last = a_(FC[p][:, b * 128:(b + 1) * 128], P1[p][:, b * 128:(b + 1) * 128], ACT.Relu,
                              bias=WSEL[q][:, b, EW + HID:NL * EW])
                last.then_inc(sem["fme1"], 1)

            def feed(s, sp, half, live):
                if live(0):
                    relu0(act, s, sp % 2)
                if live(1):
                    relu1(act, s - 1, (sp - 1) % 2, (sp - 1) % 4)
                if live(2):
                    relu2(act, s - 2, sp % 2, (sp - 2) % 4)
            steps(feed, act, GROUPS, 3, 8, 4)

        @block.vector
        def _(dve):
            v_ = nc.vector
            v_.memset(WROT[:], 0.0).then_inc(sem["zro1"], 1)
            v_.memset(WV[:], 0.0)
            v_.memset(PJ[:], 0.0)
            v_.memset(ONES[:], 1.0).then_inc(sem["zero"], 1)
            v_.memset(VB[:], 0.0).then_inc(sem["zro1"], 1)
            v_.memset(HALF[:], -0.5)
            v_.memset(NEG1[:], -1.0)
            v_.memset(OT[0][C:C + 1, :], 1.0)
            v_.memset(OT[1][C:C + 1, :], 1.0).then_inc(sem["zro1"], 1)
            dve.wait_ge(sem["zro1"], 3)
            ones = VB[:].rearrange("p (a c) -> p a c", c=18)
            v_.memset(ones[0:64, :, 8:9], 1.0)
            v_.memset(ones[64:128, :, 17:18], 1.0).then_inc(sem["zro1"], 1)
            diagonal(dve, v_.tensor_copy, 1)
            dve.wait_ge(sem["lds"], 16 * 13)
            v_.memset(BVB[:], 1.0).then_inc(sem["setd"], 1)
            dve.wait_ge(sem["setd"], 1)
            v_.tensor_scalar(BVB[:], BVB[:], BV[:, 0:1], None, ALU.mult).then_inc(sem["bvb"], 1)
            dve.wait_ge(sem["qbe"], 1)
            for v in range(1, 16, 2):
                dve.wait_ge(sem["qkp1"], v // 2 + 1)
                half, pos = v // 8, v % 8
                for qk, dst in ((0, Q2), (1, K2)):
                    d = dst[64 * half:64 * half + 64, :].rearrange("p (w r c) -> p w r c", r=8, c=8)
                    d = d[:, :, pos, :] if half == 0 else d[:, :, :, pos]
                    v_.tensor_scalar(d, v3(PQK[v % 4][64 * qk:64 * qk + 64, :], 8),
                                     QB[64 * qk:64 * qk + 64, v:v + 1], None, ALU.add).then_inc(sem["qke1"], 1)
            dve.wait_ge(sem["wsb"], 3)
            v_.tensor_scalar(WS[C:C + 1, 0:512], TP[C:C + 1, 0:512], 1.0, None, ALU.add)
            v_.tensor_copy(WS[C:C + 1, 512:1024], CX[C:C + 1, 0:512])
            v_.tensor_copy(WS[C:C + 1, 1024:WCOLS], XB[C:C + 1, 0:WCOLS - 1024])
            v_.tensor_scalar(WS[0:C, :], WS[0:C, :], LNG[:, 0:1], None, ALU.mult).then_inc(sem["wss"], 1)
            dve.wait_ge(sem["lde"], 112)
            dve.wait_ge(sem["ldp"], 48)
            for l in range(NL):
                last = v_.tensor_tensor(SHR[:, l * EW:l * EW + HID], SHR[:, l * EW:l * EW + HID], IDN[:], ALU.add)
            last.then_inc(sem["shi"], 1)
            dve.wait_ge(sem["pbe"], 1)

            def rowmax(dve, n, p, w):
                dve.wait_ge(sem[f"sc{w}"], n + 1)
                v_.tensor_reduce(NMX[w][:], v3(S[w][:], NTOK), AX.X, ALU.max, negate=True).then_inc(sem[f"mx{w}"], 1)

            cx = CX[:, 0:144].rearrange("p (a c) -> p a c", c=9)

            def denominators(dve, n, p):
                dve.wait_ge(sem["pv1"], n + 1)
                v_.reciprocal(RDEN[:], cx[:, :, 8]).then_inc(sem["rd"], 1)

            def ctx_norm(dve, n, p):
                dve.wait_ge(sem["rd"], n + 1)
                want(dve, "ctp", n)
                v_.tensor_tensor(v3(CT[:], 8), cx[:, :, 0:8], over(RDEN[:], 8), ALU.mult).then_inc(sem["cx"], 1)

            def stats1(dve, n, p):
                dve.wait_ge(sem["pj"], n + 1)
                for t in range(2):
                    last = v_.bn_stats(ST1[:, 6 * t:6 * t + 6], CX[:, 256 + 64 * t:320 + 64 * t])
                last.then_inc(sem["bs1"], 1)

            def mean_var1(dve, n, p):
                dve.wait_ge(sem["pbe"], 1)
                dve.wait_ge(sem["bs1"], n + 1)
                for t in range(2):
                    last = v_.bn_aggr(MV1[:, 2 * t:2 * t + 2], ST1[:, 6 * t:6 * t + 6])
                last.then_inc(sem["bv1"], 1)

            def radicand1(dve, n, p):
                dve.wait_ge(sem["bv1"], n + 1)
                want(dve, "rs1", n)
                mv, pw = v3(MV1[:], 2), v3(PW1[:], 2)
                v_.tensor_scalar(pw[:, :, 0], mv[:, :, 1], 1.0 + EPS, EPS * EPS, ALU.mult, ALU.add)
                v_.tensor_scalar(pw[:, :, 1], mv[:, :, 1], EPS, None, ALU.add).then_inc(sem["pw1"], 1)

            def shift1(dve, n, p):
                dve.wait_ge(sem["rs1"], n + 1)
                want(dve, "oh", n)
                want(dve, "res", n)
                mv, rs = v3(MV1[:], 2), v3(RS1[:], 2)
                v_.tensor_scalar(RA[:], rs[:, :, 1], 1.0, None, ALU.add)
                v_.scalar_tensor_tensor(v3(NB1[:], 2), mv[:, :, 0:1].to_broadcast([128, 2, 2]), -1.0, rs,
                                        ALU.mult, ALU.mult).then_inc(sem["nb1"], 1)

            def rk_max(dve, n, p):
                for t in range(2):
                    dve.wait_ge(sem[f"grk{t}"], n + 1)
                    last = v_.tensor_reduce(MR[:, t * RH:(t + 1) * RH], v3(G[t][:, 0:RW], RD), AX.X, ALU.max)
                last.then_inc(sem["mr"], 1)

            def rk_sub(dve, n, p):
                dve.wait_ge(sem["mr"], n + 1)
                want(dve, "pq", n - 1)
                for t in range(2):
                    v_.tensor_tensor(v3(RK[p][:, t * RW:(t + 1) * RW], RD), v3(G[t][:, 0:RW], RD),
                                     over(MR[:, t * RH:(t + 1) * RH], RD), ALU.subtract).then_inc(sem[f"rsub{t}"], 1)

            def elu(dve, n, p, t):
                dve.wait_ge(sem[f"eq{t}"], n + 1)
                want(dve, "pra", n)
                v_.scalar_tensor_tensor(QK[:, t * 512:(t + 1) * 512], G[t][:], 1.0, EQ[t][:],
                                        ALU.max, ALU.min).then_inc(sem[f"el{t}"], 1)

            def qk_sums(dve, n, p):
                dve.wait_ge(sem["el0"], n + 1)
                dve.wait_ge(sem["el1"], n + 1)
                want(dve, "rc", n)
                v_.tensor_reduce(SM[:, 0:32], v3(QK[:], RD), AX.X, ALU.add).then_inc(sem["sq"], 1)

            def rk_sums(dve, n, p):
                dve.wait_ge(sem["rk0"], n + 1)
                dve.wait_ge(sem["rk1"], n + 1)
                want(dve, "rc", n)
                v_.tensor_reduce(SM[:, 32:48], v3(RK[p][:], RD), AX.X, ALU.add).then_inc(sem["sr"], 1)

            def strengths(dve, n, p):
                dve.wait_ge(sem["th"], n + 1)
                want(dve, "n1", n)
                v_.tensor_scalar(BE[:], TH[:], 0.5, 0.5, ALU.mult, ALU.add).then_inc(sem["be"], 1)

            def inverses(dve, n, p):
                dve.wait_ge(sem["sq"], n + 1)
                dve.wait_ge(sem["sr"], n + 1)
                want(dve, "n1", n)
                v_.reciprocal(RC[:], SM[:]).then_inc(sem["rc"], 1)

            def dots(dve, n, p):
                dve.wait_ge(sem["pra"], n + 1)
                dve.wait_ge(sem["prr"], n + 1)
                want(dve, "n1", n)
                v_.tensor_reduce(DT[:], v3(PR[:], RD), AX.X, ALU.add).then_inc(sem["rp"], 1)

            be = BE[:].rearrange("p (t k h) -> p t k h", t=2, k=2)
            rc, dt, nm = v3(RC[:], 8), v3(DT[:], 8), v3(NM[:], 8)

            def coef(p):
                return CF[p][:].rearrange("p (t k h) -> p t k h", t=2, k=2)

            def coefs1(dve, n, p):
                dve.wait_ge(sem["rp"], n + 1)
                dve.wait_ge(sem["rc"], n + 1)
                dve.wait_ge(sem["be"], n + 1)
                want(dve, "hm2", n - 1)
                v_.tensor_tensor(nm[:, 0:2], dt[:, 0:2], rc[:, 2:4], ALU.mult)
                v_.tensor_tensor(nm[:, 2:4], dt[:, 2:4], rc[:, 0:3:2], ALU.mult)
                v_.tensor_tensor(nm[:, 4], dt[:, 4], rc[:, 5], ALU.mult)
                v_.tensor_tensor(v3(BK[:], 8), be[:, :, 0, :], rc[:, 1:4:2], ALU.mult)
                v_.tensor_tensor(v3(UU[p][:], 8), be[:, :, 1, :], rc[:, 4:6], ALU.mult).then_inc(sem["n1"], 1)
                v_.tensor_scalar(CC[p][:, 8:16], be[:, 0, 1, :], 1.0 / RD, None, ALU.mult)

            def coefs2(dve, n, p):
                dve.wait_ge(sem["n1"], n + 1)
                v_.tensor_tensor(CC[p][:, 0:8], nm[:, 2], BK[:, 0:8], ALU.mult).then_inc(sem["cc"], 1)
                v_.tensor_tensor(nm[:, 0:2], nm[:, 0:2], BK[:, 0:8].unsqueeze(1).to_broadcast([128, 2, 8]), ALU.mult)
                v_.tensor_tensor(coef(p)[:, 1, 0, :], nm[:, 3], BK[:, 8:16], ALU.mult).then_inc(sem["n2"], 1)
                v_.tensor_tensor(GG[p][:], nm[:, 4], UU[p][:, 0:8], ALU.mult)

            def coefs3(dve, n, p):
                dve.wait_ge(sem["n2"], n + 1)
                v_.tensor_tensor(TA[:], coef(p)[:, 1, 0, :], nm[:, 1], ALU.mult).then_inc(sem["n3"], 1)

            def coefs4(dve, n, p):
                dve.wait_ge(sem["n3"], n + 1)
                v_.tensor_tensor(coef(p)[:, 0, 0, :], nm[:, 0], TA[:], ALU.subtract).then_inc(sem["cf0"], 1)

            def h_max(dve, n, p):
                dve.wait_ge(sem["h1"], n + 1)
                v_.tensor_reduce(MH[:], v3(H1[:], RD), AX.X, ALU.max).then_inc(sem["mh"], 1)

            def h_query(dve, n, p):
                dve.wait_ge(sem["mh"], n + 1)
                want(dve, "qr", n)
                v_.tensor_tensor(v3(QX[:], RD), v3(H1[:], RD), over(MH[:], RD),
                                 ALU.subtract).then_inc(sem["qx"], 1)

            def query_dots(dve, n, p):
                dve.wait_ge(sem["pq"], n + 1)
                want(dve, "rq", n)
                v_.tensor_reduce(DQ[:], v3(PQ[:], RD), AX.X, ALU.add).then_inc(sem["dq"], 1)

            def query1(dve, n, p):
                dve.wait_ge(sem["dq"], n + 1)
                v_.reciprocal(RQ[:], DQ[:, 0:8])
                v_.tensor_tensor(TU[:], UU[p][:], DQ[:, 8:24], ALU.mult).then_inc(sem["rq"], 1)

            def query2(dve, n, p):
                dve.wait_ge(sem["rq"], n + 1)
                v_.tensor_tensor(v3(TU[:], 8), v3(TU[:], 8), RQ[:].unsqueeze(1).to_broadcast([128, 2, 8]),
                                 ALU.mult).then_inc(sem["t1"], 1)

            def query3(dve, n, p):
                dve.wait_ge(sem["t1"], n + 1)
                dve.wait_ge(sem["cf0"], n + 1)
                v_.tensor_tensor(TB[:], TU[:, 8:16], GG[p][:], ALU.mult).then_inc(sem["t2"], 1)
                v_.tensor_copy(coef(p)[:, 1, 1, :], TU[:, 8:16])

            def query4(dve, n, p):
                dve.wait_ge(sem["t2"], n + 1)
                v_.tensor_tensor(coef(p)[:, 0, 1, :], TU[:, 0:8], TB[:], ALU.subtract).then_inc(sem["cf1"], 1)

            def stats2(dve, n, p):
                dve.wait_ge(sem["ow"], n + 1)
                for t in range(2):
                    last = v_.bn_stats(ST2[:, 6 * t:6 * t + 6], XB[:, 64 * t:64 * t + 64])
                last.then_inc(sem["bs2"], 1)

            def mean_var2(dve, n, p):
                dve.wait_ge(sem["pbe"], 1)
                dve.wait_ge(sem["bs2"], n + 1)
                for t in range(2):
                    last = v_.bn_aggr(MV2[:, 2 * t:2 * t + 2], ST2[:, 6 * t:6 * t + 6])
                last.then_inc(sem["bv2"], 1)

            def radicand2(dve, n, p):
                dve.wait_ge(sem["bv2"], n + 1)
                want(dve, "rs2", n)
                v_.tensor_scalar(PW2[:], v3(MV2[:], 2)[:, :, 1], EPS, None, ALU.add).then_inc(sem["pw2"], 1)

            def shift2(dve, n, p):
                dve.wait_ge(sem["rs2"], n + 1)
                want(dve, "zz", n)
                v_.scalar_tensor_tensor(NB2[:], v3(MV2[:], 2)[:, :, 0], -1.0, RS2[:], ALU.mult,
                                        ALU.mult).then_inc(sem["nb2"], 1)

            def step(s, sp, half, live):
                if live(4):
                    elu(dve, s - 4, sp, 0)
                if live(3):
                    denominators(dve, s - 3, 1 - sp)
                    ctx_norm(dve, s - 3, 1 - sp)
                if live(5):
                    query_dots(dve, s - 5, 1 - sp)
                if live(1):
                    rowmax(dve, s - 1, 1 - sp, 0)
                if live(3):
                    stats1(dve, s - 3, 1 - sp)
                if live(5):
                    query1(dve, s - 5, 1 - sp)
                if live(3):
                    mean_var1(dve, s - 3, 1 - sp)
                if live(6):
                    shift2(dve, s - 6, sp)
                if live(5):
                    query2(dve, s - 5, 1 - sp)
                if live(3):
                    radicand1(dve, s - 3, 1 - sp)
                if live(4):
                    qk_sums(dve, s - 4, sp)
                if live(5):
                    query3(dve, s - 5, 1 - sp)
                if live(3):
                    shift1(dve, s - 3, 1 - sp)
                if live(5):
                    query4(dve, s - 5, 1 - sp)
                if live(4):
                    inverses(dve, s - 4, sp)
                    dots(dve, s - 4, sp)
                    coefs1(dve, s - 4, sp)
                    coefs2(dve, s - 4, sp)
                if live(3):
                    rk_max(dve, s - 3, 1 - sp)
                    rk_sub(dve, s - 3, 1 - sp)
                if live(4):
                    coefs3(dve, s - 4, sp)
                if live(1):
                    rowmax(dve, s - 1, 1 - sp, 1)
                if live(4):
                    h_max(dve, s - 4, sp)
                    h_query(dve, s - 4, sp)
                if live(3):
                    rk_sums(dve, s - 3, 1 - sp)
                if live(5):
                    stats2(dve, s - 5, 1 - sp)
                if live(4):
                    coefs4(dve, s - 4, sp)
                if live(5):
                    mean_var2(dve, s - 5, 1 - sp)
                    radicand2(dve, s - 5, 1 - sp)
                if live(3):
                    strengths(dve, s - 3, 1 - sp)
                    elu(dve, s - 3, 1 - sp, 1)
            steps(step, dve)

            def select(dve, g, q):
                want(dve, "fme1", g - 3)
                for b in range(BLK // 2, BLK):
                    e = dve.value_load(ROUTE[0:1, bass.ds(g * BLK + b, 1)], min_val=0, max_val=NE - 1)
                    last = v_.tensor_tensor(WSEL[q][:, b, :], EXP[:, bass.ds(e * (NL * EW), NL * EW)], SHR[:], ALU.add)
                last.then_inc(sem["fsel1"], 1)

            def finish(dve, g, p, pair):
                dve.wait_ge(sem["fo"], g + 1)
                want(dve, f"fst{p}", pair * 16)
                y = HZT[64:128, bass.ds(g * 512, 512)].rearrange("p (w n) -> p w n", w=8)
                for b in range(BLK):
                    last = v_.scalar_tensor_tensor(
                        v3(FO[p][:, b * 128:(b + 1) * 128], 16), v3(PO[p][64:128, b * 128:(b + 1) * 128], 16),
                        BO[64:128, 0:1], y[:, :, b * 16:(b + 1) * 16], ALU.add, ALU.add)
                last.then_inc(sem["foe"], 1)

            def feed(s, sp, half, live):
                if live(0):
                    select(dve, s, sp)
                if live(3):
                    finish(dve, s - 3, (sp - 3) % 2, half * 2 + (sp - 3) // 2)
            dve.wait_ge(sem["hz"], TILES)
            steps(feed, dve, GROUPS, 3, 8, 4)

        @block.tensor
        def _(pe):
            mm = nc.tensor.matmul
            tr = nc.tensor.transpose
            pe.wait_ge(sem["ldw"], 48)
            for t in range(2):
                for half in range(2):
                    mm(G[half][64 * t:64 * t + 64, :], WQK[:], ROT[:, half * 512:(half + 1) * 512],
                       start=True, stop=True).then_inc(sem["wr"], 1)
            for v in range(16):
                for qk in range(2):
                    for t in range(2):
                        row = qk * 64 + t * 32
                        last = mm(XA[row:row + 32, v:v + 1], ROT[:, v * 64 + qk * 32:v * 64 + qk * 32 + 32], BQK[:, 0:1],
                                  start=True, stop=True)
            last.then_inc(sem["qbm"], 1)
            pe.wait_ge(sem["wre"], 4)
            pe.wait_ge(sem["ldx"], 16)
            x5 = X2[:].rearrange("p (w r c) -> p w r c", r=8, c=8)
            for v in range(16):
                half, pos = v // 8, v % 8
                want(pe, f"qke{v % 2}", 2 * (v // 2 - 1))
                rhs = x5[:, :, pos, :] if half == 0 else x5[:, :, :, pos]
                mm(PQK[v % 4][:], WROT[:, v * 128:(v + 1) * 128], rhs, start=True, stop=True)\
                    .then_inc(sem[f"qkp{v % 2}"], 1)
            pe.wait_ge(sem["lds"], 16 * 13)
            for i, (b_, lo, hi) in enumerate(((TP, 0, 512), (CX, 512, 1024), (XB, 1024, WCOLS))):
                mm(b_[C:C + 1, 0:hi - lo], LNB[:, 0:1], WS[0:C, lo:hi], start=True, stop=True).then_inc(sem["wsb"], 1)
            pe.wait_ge(sem["bvb"], 1)
            pe.wait_ge(sem["zero"], 1)
            pe.wait_ge(sem["qbe"], 1)
            mm(XA[:, 0:C], BVB[:], PJ[0:C, 0:C], start=True, stop=False)
            mm(XA[:, 0:C], ONES[:], PROWB[:], start=False, stop=True).then_inc(sem["pbm"], 1)
            pe.wait_ge(sem["zro1"], 4)
            pe.wait_ge(sem["wss"], 1)
            pe.wait_ge(sem["ldp"], 48)

            def values(pe, n, p, pair):
                pe.wait_ge(sem[f"xt{p}"], pair * 16 + 16)
                want(pe, "ot", n)
                for w in range(2):
                    for e in range(2):
                        last = mm(XA[64 * e:64 * e + 64, w * 64:(w + 1) * 64], XT[p][:, w * 64:(w + 1) * 64],
                                  WV[:, e * 64:(e + 1) * 64], start=True, stop=True)
                last.then_inc(sem["vp"], 1)

            def scores(pe, n, p, w):
                pe.wait_ge(sem["qw"], n + 1)
                pe.wait_ge(sem[f"kb{w}"], n + 1)
                want(pe, f"ex{w}", n)
                mm(S[w][:], QW[p][:, w * 128:(w + 1) * 128], KB[p][w][:], start=True, stop=True)\
                    .then_inc(sem[f"sc{w}"], 1)

            def probsT(pe, n, p, w):
                pe.wait_ge(sem[f"ex{w}"], n + 1)
                want(pe, f"pt{1 - w}", n + w)
                for j in range(4):
                    last = tr(TP[:, j * 128:(j + 1) * 128], SX[w][:, j * 128:(j + 1) * 128], IDN[:])
                last.then_inc(sem[f"tp{w}"], 1)

            vb = VB[:].rearrange("p (w t j c) -> p w t j c", w=2, t=2, j=4)
            cx = CX[:, 0:144].rearrange("p (t j c) -> p t j c", t=2, j=4)

            def attend(pe, n, p, w):
                pe.wait_ge(sem[f"pt{w}"], n + 1)
                if w == 0:
                    pe.wait_ge(sem["vb"], n + 1)
                    want(pe, "res", n)
                for t in range(2):
                    for j in range(4):
                        last = mm(cx[64 * w:64 * w + 64, t, j, :], PT[w][:, j * 128 + t * 64:j * 128 + t * 64 + 64],
                                  vb[:, w, t, j, :], start=True, stop=True)
                last.then_inc(sem[f"pv{w}"], 1)

            def ctxT(pe, n, p):
                pe.wait_ge(sem["cx"], n + 1)
                tr(XA[:, 128:256], CT[:], IDN[:]).then_inc(sem["ctp"], 1)

            def project(pe, n, p):
                mm(CX[:, 256:384], ONES[:], PBIAS[0:1, :], start=True, stop=False)
                pe.wait_ge(sem["ctt"], n + 1)
                mm(CX[:, 256:384], CTT[:], PJ[:], start=False, stop=True).then_inc(sem["pj"], 1)

            def obsT(pe, n, p):
                pe.wait_ge(sem["ldp"], 48)
                pe.wait_ge(sem["oh"], n + 1)
                for t in range(2):
                    last = tr(XA[0:C, t * 128:(t + 1) * 128], OH[:, t * C:(t + 1) * C], IDN[:])
                last.then_inc(sem["otp"], 1)

            def slow(pe, n, p, what, t):
                lo, wide = {"rk": (CRK, RW + 2 * RH), "qk": (CQK, 512), "v": (CV, 512)}[what]
                if what == "rk":
                    pe.wait_ge(sem["ot"], n + 1)
                    want(pe, f"vv{t}", n)
                elif what == "qk":
                    pe.wait_ge(sem[f"rsub{t}"], n + 1)
                    pe.wait_ge(sem["th"], n + 1)
                else:
                    pe.wait_ge(sem[f"el{t}"], n + 1)
                mm(G[t][:, 0:wide], OT[p][:, t * 128:(t + 1) * 128], WS[:, lo:lo + wide], start=True, stop=True)\
                    .then_inc(sem[f"g{what}{t}"], 1)

            def hT(pe, n, p):
                pe.wait_ge(sem["hm2"], n + 1)
                pe.wait_ge(sem["h1"], n + 1)
                want(pe, "hz", n)
                for c in range(2):
                    tr(XB[:, c * 256:c * 256 + 128], H1[:, c * 128:(c + 1) * 128], IDN[:])
                for c in range(2):
                    for j in range(4):
                        last = mm(XB[:, c * 256 + 128:c * 256 + 256], HM2[:, j * RW + c * 128:j * RW + c * 128 + 128],
                                  IDN[:], start=(j == 0), stop=(j == 3))
                last.then_inc(sem["htp"], 1)

            def output(pe, n, p):
                pe.wait_ge(sem["res"], n + 1)
                pe.wait_ge(sem["ht"], n + 1)
                mm(XB[:, 0:128], IDN[:], RES[p][:], start=True, stop=False)
                for t in range(2):
                    for c in range(2):
                        k = (c * 2 + t) * 128
                        last = mm(XB[:, t * C:(t + 1) * C], HT[:, k:k + 128], OW[:, c * C:(c + 1) * C],
                                  start=False, stop=(t == 1 and c == 1))
                last.then_inc(sem["ow"], 1)

            def hzT(pe, n, p):
                pe.wait_ge(sem["zz"], n + 1)
                pe.wait_ge(sem["yy"], n + 1)
                for t in range(2):
                    last = tr(XB[:, 256 + t * 128:384 + t * 128], HZ[:, t * 128:(t + 1) * 128], IDN[:])
                last.then_inc(sem["ztp"], 1)

            def step(s, sp, half, live):
                if live(3):
                    attend(pe, s - 3, 1 - sp, 0)
                    attend(pe, s - 3, 1 - sp, 1)
                if live(1):
                    scores(pe, s - 1, 1 - sp, 0)
                if live(3):
                    ctxT(pe, s - 3, 1 - sp)
                    project(pe, s - 3, 1 - sp)
                if live(2):
                    probsT(pe, s - 2, sp, 0)
                if live(4):
                    slow(pe, s - 4, sp, "v", 0)
                    slow(pe, s - 4, sp, "v", 1)
                if live(2):
                    probsT(pe, s - 2, sp, 1)
                if live(1):
                    scores(pe, s - 1, 1 - sp, 1)
                if live(3):
                    obsT(pe, s - 3, 1 - sp)
                if live(6):
                    hzT(pe, s - 6, sp)
                if live(3):
                    slow(pe, s - 3, 1 - sp, "rk", 0)
                    slow(pe, s - 3, 1 - sp, "rk", 1)
                if live(5):
                    hT(pe, s - 5, 1 - sp)
                if live(2):
                    values(pe, s - 2, sp, half + (sp - 2) // 2)
                if live(3):
                    slow(pe, s - 3, 1 - sp, "qk", 1)
                if live(5):
                    output(pe, s - 5, 1 - sp)
                if live(3):
                    slow(pe, s - 3, 1 - sp, "qk", 0)
            steps(step, pe)

            def hidden(pe, g, p):
                want(pe, "fhe", g - 1)
                mm(PH[p][:], WI[:], HZT[0:C, bass.ds(g * 512, 512)], start=True, stop=True).then_inc(sem["fh"], 1)

            def expert0(pe, g, p, q):
                pe.wait_ge(sem["fhe"], g + 1)
                pe.wait_ge(sem["fsel0"], g + 1)
                pe.wait_ge(sem["fsel1"], g + 1)
                want(pe, "fme0", g - 1)
                fa = FA[p].rearrange("p (w n) -> p w n", w=8)
                for b in range(BLK):
                    last = mm(v3(P0[p][:, b * 128:(b + 1) * 128], 16), WSEL[q][:, b, 0:HID],
                              fa[:, :, b * 16:(b + 1) * 16], start=True, stop=True)
                last.then_inc(sem["fm0"], 1)

            def expert1(pe, g, p, q):
                pe.wait_ge(sem["fme0"], g + 1)
                want(pe, "fme1", g - 1)
                for b in range(BLK):
                    last = mm(P1[p][:, b * 128:(b + 1) * 128], WSEL[q][:, b, EW:EW + HID],
                              FB[p][:, b * 128:(b + 1) * 128], start=True, stop=True)
                last.then_inc(sem["fm1"], 1)

            def result(pe, g, p):
                pe.wait_ge(sem["fme1"], g + 1)
                want(pe, "foe", g - 1)
                mm(PO[p][64:128, :], WO[:], FC[p], start=True, stop=True).then_inc(sem["fo"], 1)

            def feed(s, sp, half, live):
                if live(0):
                    hidden(pe, s, sp % 2)
                if live(1):
                    expert0(pe, s - 1, (sp - 1) % 2, (sp - 1) % 4)
                if live(2):
                    expert1(pe, s - 2, sp % 2, (sp - 2) % 4)
                if live(3):
                    result(pe, s - 3, (sp - 3) % 2)
            pe.wait_ge(sem["hz"], TILES)
            pe.wait_ge(sem["lde"], 112)
            steps(feed, pe, GROUPS, 3, 8, 4)


def _rotations():
    rot = np.zeros((128, 16, 2, NH * 4), np.float32)
    half = HD // 2
    inv = 1.0 / 10000.0 ** (np.arange(0, half, 2, dtype=np.float32) / half)
    for v in range(16):
        for qk in range(2):
            scale = HD ** -0.5 if qk == 0 else 1.0
            for h in range(NH):
                for f in range(2):
                    a = np.float32(v % 8) * inv[f]
                    c, s = scale * np.cos(a), scale * np.sin(a)
                    src = qk * 64 + h * HD + (v // 8) * half + 2 * f
                    dst = h * 4 + 2 * f
                    rot[src, v, qk, dst] = c
                    rot[src + 1, v, qk, dst] = -s
                    rot[src, v, qk, dst + 1] = s
                    rot[src + 1, v, qk, dst + 1] = c
    return rot.reshape(128, 16 * 64)


def kernel(x, L0_tok_qkv_w, L0_tok_qkv_b, L0_tok_proj_w, L0_tok_proj_b, L0_attn_slow_W, L0_attn_out_W,
           L0_attn_ln_g, L0_attn_ln_b, L0_ffn_route_id, L0_ffn_Wi, L0_ffn_bi, L0_ffn_Wr, L0_ffn_br,
           L0_ffn_Ws, L0_ffn_bs, L0_ffn_Wo, L0_ffn_bo):
    import concourse.bacc as bacc
    from concourse.bass_utils import run_bass_kernel_spmd

    x, qkv_w, qkv_b, proj_w, proj_b, slow, outw, ln_g, ln_b, route, Wi, bi, Wr, br, Ws, bs, Wo, bo = (
        np.asarray(a) for a in (x, L0_tok_qkv_w, L0_tok_qkv_b, L0_tok_proj_w, L0_tok_proj_b, L0_attn_slow_W,
                                L0_attn_out_W, L0_attn_ln_g, L0_attn_ln_b, L0_ffn_route_id, L0_ffn_Wi,
                                L0_ffn_bi, L0_ffn_Wr, L0_ffn_br, L0_ffn_Ws, L0_ffn_bs, L0_ffn_Wo, L0_ffn_bo))
    x2 = x.reshape(B, 8, 8, 8, 8, C).transpose(0, 5, 1, 3, 2, 4).reshape(B * C, TOK)
    wv = qkv_w[128:192].reshape(4, 2, HD, C).transpose(3, 1, 0, 2).reshape(C, C)
    sw = slow.reshape(RH, 5 * RD + 2, C)
    fields = [sw[:, i * RD:(i + 1) * RD].reshape(RW, C) for i in range(5)]
    slowT = np.concatenate([fields[0], fields[1], fields[2], fields[4], fields[3], sw[:, 5 * RD], sw[:, 5 * RD + 1]]).T
    experts = np.concatenate([Wr.transpose(3, 1, 0, 2), br.transpose(2, 1, 0)[..., None]], -1).reshape(HID, -1)
    shared = np.concatenate([Ws[:, 0].transpose(2, 0, 1), bs[:, 0].T[..., None]], -1).reshape(HID, -1)
    p = np.arange(128)
    ins = dict(
        x2=x2, wqk=qkv_w[0:128], wv=wv, bqk=qkv_b[0:128, None], bv=qkv_b[128:192, None], projT=proj_w.T,
        projb=proj_b[None], rot=_rotations(),
        mask_img=((p[:, None] // 32) % 2 == np.arange(2)).astype(np.float32),
        mask_head=((p[:, None] % 32) // 4 == np.arange(NH)).astype(np.float32),
        ident_in=np.eye(128, dtype=np.float32), slowT=slowT, outT=outw.T, ln_g=ln_g[:, None], ln_b=ln_b[:, None],
        route=route[None], wiT=Wi.T, bi=bi[:, None], experts=experts, shared=shared, woT=Wo.T, bo=bo[:, None])
    nc = bacc.Bacc("TRN2", target_bir_lowering=False, num_devices=1)
    arrays, args = {}, []
    for name, a in ins.items():
        a = np.ascontiguousarray(a)
        arrays[f"in_{name}"] = a
        args.append(nc.dram_tensor(f"in_{name}", a.shape, mybir.dt.from_np(a.dtype), kind="ExternalInput").ap())
    out = nc.dram_tensor("out_0", (GROUPS, C, 512), F32, kind="ExternalOutput").ap()
    vit_tower(nc, *args, out)
    r = run_bass_kernel_spmd(nc, [arrays], core_ids=[0])
    y = r.results[0]["out_0"]
    y = y.reshape(B, 8, C, BLK, 8, 2, 8).transpose(0, 1, 3, 5, 4, 6, 2)
    return np.ascontiguousarray(y.reshape(B, TOK, C))
```
